# Optimizing a Trainium2 kernel written in Bass

```python
import numpy as np
import jax
import jax.numpy as jnp

def _softmax(x, axis=-1):
    return jax.nn.softmax(x, axis=axis)

def _gelu(x):
    return jax.nn.gelu(x, approximate=True)

def _silu(x):
    return jax.nn.silu(x)

def _sigmoid(x):
    return jax.nn.sigmoid(x)

def _layernorm(x, axis=-1, eps=1e-05):
    m = jnp.mean(x, axis=axis, keepdims=True)
    v = jnp.var(x, axis=axis, keepdims=True)
    return (x - m) / jnp.sqrt(v + eps)

def _scatter_add(tgt, idx, src, axis=0):
    return tgt.at[idx].add(src)

def _segment_sum(src, seg, n):
    return jax.ops.segment_sum(src, seg, n)
kernel_name = 'mk_gnn_resnorm_d4_gnn_r16_336a2b'

def setup_inputs(seed: int=0):
    np.random.seed(seed)
    _w = jnp.asarray

    def _rec_inputs():
        import jax
        import jax.numpy as jnp
        _gk = jax.random.key(seed)
        x = -0.000202 + 1 * jax.random.normal(jax.random.fold_in(_gk, 1), (6250, 64), jnp.float32)
        _s = jax.random.randint(jax.random.fold_in(_gk, 2), (100000,), 0, 6250, jnp.int32)
        _d = jax.random.randint(jax.random.fold_in(_gk, 3), (100000,), 0, 6250, jnp.int32)
        _loop = jnp.arange(6250, dtype=jnp.int32)
        src = jnp.concatenate([_s, _d, _loop])
        dst = jnp.concatenate([_d, _s, _loop])
        _o = jnp.argsort(dst, stable=True)
        src = src[_o]
        dst = dst[_o]
        edge_attr_64 = -9.77346e-05 + 0.999888 * jax.random.normal(jax.random.fold_in(_gk, 12), (206250, 64), jnp.float32)
        return (x, src, dst, edge_attr_64)
    x, src, dst, edge_attr_64 = _rec_inputs()

    def _L0_gnn_setup():
        import jax, jax.numpy as jnp
        import numpy as np
        NUM_NODES = 6250
        NUM_HYPEREDGES = 12500
        NNZ = 75000
        IN_DIM = 64
        HID_DIM = 64
        OUT_DIM = 64

        def _hypergraph_conv(x, node_idx, edge_idx, D_inv, B_inv, W, b):
            xt = x @ W
            e = B_inv[:, None] * jax.ops.segment_sum(xt[node_idx], edge_idx, num_segments=NUM_HYPEREDGES)
            out = D_inv[:, None] * jax.ops.segment_sum(e[edge_idx], node_idx, num_segments=NUM_NODES)
            return out + b
        key = jax.random.key(seed)
        k1, k2, k3, k4, k5, k6, k7, k8 = jax.random.split(key, 8)
        x = jax.random.normal(k1, (NUM_NODES, IN_DIM), dtype=jnp.float32)
        node_idx = jax.random.randint(k2, (NNZ,), 0, NUM_NODES, dtype=jnp.int64)
        edge_idx = jax.random.randint(k3, (NNZ,), 0, NUM_HYPEREDGES, dtype=jnp.int64)
        hyperedge_index = jnp.stack([node_idx, edge_idx], axis=0)
        s1 = 1.0 / np.sqrt(IN_DIM)
        s2 = 1.0 / np.sqrt(HID_DIM)
        W1 = jax.random.uniform(k4, (IN_DIM, HID_DIM), jnp.float32, -s1, s1)
        b1 = jax.random.uniform(k5, (HID_DIM,), jnp.float32, -s1, s1)
        W2 = jax.random.uniform(k6, (HID_DIM, OUT_DIM), jnp.float32, -s2, s2)
        b2 = jax.random.uniform(k7, (OUT_DIM,), jnp.float32, -s2, s2)
        return {'x': x, 'hyperedge_index': hyperedge_index, 'W1': W1, 'b1': b1, 'W2': W2, 'b2': b2}
    _L0_gnn_all = _L0_gnn_setup()
    _L0_gnn_in = {k: v for k, v in _L0_gnn_all.items() if k in ('W1', 'b1', 'W2', 'b2')}
    del _L0_gnn_all

    def _L1_gnn_setup():
        import jax, jax.numpy as jnp
        import numpy as np
        N_NODES = 3125
        N_EDGES = 50000
        D = 64
        H = 128
        key = jax.random.key(seed)
        ks = jax.random.split(key, 8)
        s = 0.05
        return {'nodes': jax.random.normal(ks[0], (N_NODES, D), jnp.float32), 'edges': jax.random.normal(ks[1], (N_EDGES, D), jnp.float32), 'We1': jax.random.normal(ks[2], (3 * D, H), jnp.float32) * s, 'be1': jnp.zeros((H,), jnp.float32), 'We2': jax.random.normal(ks[3], (H, D), jnp.float32) * s, 'be2': jnp.zeros((D,), jnp.float32), 'Wn1': jax.random.normal(ks[4], (2 * D, H), jnp.float32) * s, 'bn1': jnp.zeros((H,), jnp.float32), 'Wn2': jax.random.normal(ks[5], (H, D), jnp.float32) * s, 'bn2': jnp.zeros((D,), jnp.float32), 'senders': jax.random.randint(ks[6], (N_EDGES,), 0, N_NODES, jnp.int32), 'receivers': jax.random.randint(ks[7], (N_EDGES,), 0, N_NODES, jnp.int32)}
    _L1_gnn_all = _L1_gnn_setup()
    _L1_gnn_in = {k: v for k, v in _L1_gnn_all.items() if k in ('We1', 'be1', 'We2', 'be2', 'Wn1', 'bn1', 'Wn2', 'bn2')}
    del _L1_gnn_all

    def _L2_gnn_setup():
        import jax, jax.numpy as jnp
        import numpy as np
        N_NODES = 6250
        key = jax.random.key(seed)
        ks = jax.random.split(key, 11)
        d_in, d_out = (64, 64)
        n_edges = 100000
        x = jax.random.normal(ks[0], (N_NODES, d_in), dtype=jnp.float32)
        edge_index = jax.random.randint(ks[1], (2, n_edges), 0, N_NODES, dtype=jnp.int64)
        s = 1.0 / np.sqrt(d_in)
        return {'x': x, 'edge_index': edge_index, 'W_key': jax.random.normal(ks[2], (d_in, d_out), dtype=jnp.float32) * s, 'b_key': jax.random.normal(ks[3], (d_out,), dtype=jnp.float32) * s, 'W_query': jax.random.normal(ks[4], (d_in, d_out), dtype=jnp.float32) * s, 'b_query': jax.random.normal(ks[5], (d_out,), dtype=jnp.float32) * s, 'W_value': jax.random.normal(ks[6], (d_in, d_out), dtype=jnp.float32) * s, 'b_value': jax.random.normal(ks[7], (d_out,), dtype=jnp.float32) * s, 'W_skip': jax.random.normal(ks[8], (d_in, d_out), dtype=jnp.float32) * s, 'b_skip': jax.random.normal(ks[9], (d_out,), dtype=jnp.float32) * s}
    _L2_gnn_all = _L2_gnn_setup()
    _L2_gnn_in = {k: v for k, v in _L2_gnn_all.items() if k in ('W_key', 'b_key', 'W_query', 'b_query', 'W_value', 'b_value', 'W_skip', 'b_skip')}
    del _L2_gnn_all

    def _L3_gnn_setup():
        import jax, jax.numpy as jnp
        import numpy as np
        N_NODES = 12500
        EMBED_DIM = 64
        N_EDGES = 312500

        def _lightgcn_forward(x, edge_index):
            n = x.shape[0]
            loop = jnp.arange(n, dtype=edge_index.dtype)
            row = jnp.concatenate([edge_index[0], loop])
            col = jnp.concatenate([edge_index[1], loop])
            w = jnp.ones(row.shape[0], dtype=x.dtype)
            deg = jax.ops.segment_sum(w, row, num_segments=n)
            inv_deg = 1.0 / (deg + 1e-08)
            w = w * inv_deg[row]
            deg2 = jax.ops.segment_sum(w, row, num_segments=n)
            inv_sqrt = jnp.where(deg2 > 0, jax.lax.rsqrt(deg2 + 1e-08), 0.0)
            w = inv_sqrt[row] * w * inv_sqrt[col]
            h = jax.ops.segment_sum(w[:, None] * x[col], row, num_segments=n)
            return h
        key = jax.random.key(seed)
        k1, k2 = jax.random.split(key)
        x = jax.random.normal(k1, (N_NODES, EMBED_DIM), dtype=jnp.float32)
        edge_index = jax.random.randint(k2, (2, N_EDGES), 0, N_NODES, dtype=jnp.int64)
        return {'x': x, 'edge_index': edge_index}
    _L3_gnn_all = _L3_gnn_setup()
    _L3_gnn_in = {k: v for k, v in _L3_gnn_all.items() if k in ()}
    del _L3_gnn_all
    return {'x': x, 'src': src, 'dst': dst, 'edge_attr_64': edge_attr_64, 'L0_gnn_W1': _L0_gnn_in['W1'], 'L0_gnn_b1': _L0_gnn_in['b1'], 'L0_gnn_W2': _L0_gnn_in['W2'], 'L0_gnn_b2': _L0_gnn_in['b2'], 'L1_gnn_We1': _L1_gnn_in['We1'], 'L1_gnn_be1': _L1_gnn_in['be1'], 'L1_gnn_We2': _L1_gnn_in['We2'], 'L1_gnn_be2': _L1_gnn_in['be2'], 'L1_gnn_Wn1': _L1_gnn_in['Wn1'], 'L1_gnn_bn1': _L1_gnn_in['bn1'], 'L1_gnn_Wn2': _L1_gnn_in['Wn2'], 'L1_gnn_bn2': _L1_gnn_in['bn2'], 'L2_gnn_W_key': _L2_gnn_in['W_key'], 'L2_gnn_b_key': _L2_gnn_in['b_key'], 'L2_gnn_W_query': _L2_gnn_in['W_query'], 'L2_gnn_b_query': _L2_gnn_in['b_query'], 'L2_gnn_W_value': _L2_gnn_in['W_value'], 'L2_gnn_b_value': _L2_gnn_in['b_value'], 'L2_gnn_W_skip': _L2_gnn_in['W_skip'], 'L2_gnn_b_skip': _L2_gnn_in['b_skip']}

def reference(x, src, dst, edge_attr_64, L0_gnn_W1, L0_gnn_b1, L0_gnn_W2, L0_gnn_b2, L1_gnn_We1, L1_gnn_be1, L1_gnn_We2, L1_gnn_be2, L1_gnn_Wn1, L1_gnn_bn1, L1_gnn_Wn2, L1_gnn_bn2, L2_gnn_W_key, L2_gnn_b_key, L2_gnn_W_query, L2_gnn_b_query, L2_gnn_W_value, L2_gnn_b_value, L2_gnn_W_skip, L2_gnn_b_skip):
    import jax
    import jax.numpy as jnp

    def _L0_gnn_ref(x, hyperedge_index, W1, b1, W2, b2):
        import jax, jax.numpy as jnp
        import numpy as np
        NUM_NODES = 6250
        NUM_HYPEREDGES = 12500
        NNZ = 75000
        IN_DIM = 64
        HID_DIM = 64
        OUT_DIM = 64

        def _hypergraph_conv(x, node_idx, edge_idx, D_inv, B_inv, W, b):
            xt = x @ W
            e = B_inv[:, None] * jax.ops.segment_sum(xt[node_idx], edge_idx, num_segments=NUM_HYPEREDGES)
            out = D_inv[:, None] * jax.ops.segment_sum(e[edge_idx], node_idx, num_segments=NUM_NODES)
            return out + b
        node_idx = hyperedge_index[0]
        edge_idx = hyperedge_index[1]
        ones = jnp.ones((node_idx.shape[0],), dtype=x.dtype)
        D = jax.ops.segment_sum(ones, node_idx, num_segments=NUM_NODES)
        B = jax.ops.segment_sum(ones, edge_idx, num_segments=NUM_HYPEREDGES)
        D_inv = jnp.where(D > 0, 1.0 / D, 0.0)
        B_inv = jnp.where(B > 0, 1.0 / B, 0.0)
        h = jax.nn.relu(_hypergraph_conv(x, node_idx, edge_idx, D_inv, B_inv, W1, b1))
        y = _hypergraph_conv(h, node_idx, edge_idx, D_inv, B_inv, W2, b2)
        return y

    def _L1_gnn_ref(nodes, edges, We1, be1, We2, be2, Wn1, bn1, Wn2, bn2, senders, receivers):
        import jax, jax.numpy as jnp
        import numpy as np
        N_NODES = 3125
        N_EDGES = 50000
        D = 64
        H = 128
        edge_in = jnp.concatenate([edges, nodes[receivers], nodes[senders]], axis=-1)
        h = jax.nn.relu(edge_in @ We1 + be1)
        new_edges = h @ We2 + be2
        agg = jax.ops.segment_sum(new_edges, receivers, num_segments=nodes.shape[0])
        node_in = jnp.concatenate([agg, nodes], axis=-1)
        h2 = jax.nn.relu(node_in @ Wn1 + bn1)
        new_nodes = h2 @ Wn2 + bn2
        return new_nodes

    def _L2_gnn_ref(x, edge_index, W_key, b_key, W_query, b_query, W_value, b_value, W_skip, b_skip):
        import jax, jax.numpy as jnp
        import numpy as np
        N_NODES = 6250
        k = x @ W_key + b_key
        q = x @ W_query + b_query
        v = x @ W_value + b_value
        src = edge_index[0]
        dst = edge_index[1]
        gate = jax.nn.sigmoid(k[dst] + q[src])
        msg = gate * v[src]
        agg = jax.ops.segment_sum(msg, dst, num_segments=N_NODES)
        return agg + x @ W_skip + b_skip

    def _L3_gnn_ref(x, edge_index):
        import jax, jax.numpy as jnp
        import numpy as np
        N_NODES = 12500
        EMBED_DIM = 64
        N_EDGES = 312500

        def _lightgcn_forward(x, edge_index):
            n = x.shape[0]
            loop = jnp.arange(n, dtype=edge_index.dtype)
            row = jnp.concatenate([edge_index[0], loop])
            col = jnp.concatenate([edge_index[1], loop])
            w = jnp.ones(row.shape[0], dtype=x.dtype)
            deg = jax.ops.segment_sum(w, row, num_segments=n)
            inv_deg = 1.0 / (deg + 1e-08)
            w = w * inv_deg[row]
            deg2 = jax.ops.segment_sum(w, row, num_segments=n)
            inv_sqrt = jnp.where(deg2 > 0, jax.lax.rsqrt(deg2 + 1e-08), 0.0)
            w = inv_sqrt[row] * w * inv_sqrt[col]
            h = jax.ops.segment_sum(w[:, None] * x[col], row, num_segments=n)
            return h
        return _lightgcn_forward(x, edge_index)
    edge_index = jnp.stack([src, dst])
    x = _layernorm(x + _L0_gnn_ref(x, edge_index, L0_gnn_W1, L0_gnn_b1, L0_gnn_W2, L0_gnn_b2), axis=-1)
    x = _layernorm(x + _L1_gnn_ref(x, edge_attr_64, L1_gnn_We1, L1_gnn_be1, L1_gnn_We2, L1_gnn_be2, L1_gnn_Wn1, L1_gnn_bn1, L1_gnn_Wn2, L1_gnn_bn2, src, dst), axis=-1)
    x = _layernorm(x + _L2_gnn_ref(x, edge_index, L2_gnn_W_key, L2_gnn_b_key, L2_gnn_W_query, L2_gnn_b_query, L2_gnn_W_value, L2_gnn_b_value, L2_gnn_W_skip, L2_gnn_b_skip), axis=-1)
    x = _layernorm(x + _L3_gnn_ref(x, edge_index), axis=-1)
    return x

_drawn_inputs = setup_inputs


def setup_inputs(seed=0):
    import zlib

    import numpy as np

    out = dict(_drawn_inputs(seed))
    spreads = {'L1_gnn_be1': (0.0, 0.1),
     'L1_gnn_be2': (0.0, 0.1),
     'L1_gnn_bn1': (0.0, 0.304),
     'L1_gnn_bn2': (0.0, 0.1)}
    factors = {'edge_attr_64': 2.799, 'L0_gnn_W1': 47.009, 'L0_gnn_b1': 2.72, 'L2_gnn_b_skip': 4.83}
    for name, (base, spread) in spreads.items():
        noise = np.random.default_rng([zlib.crc32(name.encode()), seed]).standard_normal(out[name].shape)
        drawn = base * np.exp(spread * noise) if base else spread * noise
        out[name] = jnp.asarray(drawn.astype(out[name].dtype))
    for name, factor in factors.items():
        out[name] = (out[name] * factor).astype(out[name].dtype)
    return out
```

```python
import concourse.bass as bass
from concourse import mybir
from contextlib import ExitStack


N = 6250
E = 206250
D = 64
H = 128
P = 128
NB = -(-N // P)
NP = NB * P
FULL = N // NB
REST = N - FULL * NB
GROUP = 7
STEPS = NB // GROUP
EP = 125
ET = E // EP
EPS = 1e-5
DEG_EPS = 1e-8


def build(nc, x, src, dst, feat, W1, b1, W2, b2, We1, be1, We2, be2, Wn1, bn1, Wn2, bn2,
          Wk, bk, Wq, bq, Wv, bv, Ws, bs, out):
    f32 = mybir.dt.float32
    i32 = mybir.dt.int32
    u32 = mybir.dt.uint32
    ALU = mybir.AluOpType
    ACT = mybir.ActivationFunctionType
    AX = mybir.AxisListType

    ctx = ExitStack()
    with ctx:
        def sb(name, shape, dt=f32):
            return ctx.enter_context(nc.sbuf_tensor(name, shape, dt))

        def sem(name):
            return ctx.enter_context(nc.semaphore(name))

        W_TAB = [D + 1, D + 1, D, D, H, D, D]
        tab = [nc.dram_tensor(f"tab{k}", (NP, w), f32, kind="Internal").ap()
               for k, w in enumerate([D + 1, D + 1, D, D, H, D, D])]
        tab_src = {4: nc.dram_tensor("tab_l1_src", (NP, H), f32, kind="Internal").ap(),
                   5: nc.dram_tensor("tab_l2_src", (NP, H), f32, kind="Internal").ap()}
        acc = [nc.dram_tensor(f"acc{k}", (NP + P, w), f32, kind="Internal").ap() for k, w in enumerate(W_TAB)]

        XR = sb("XR", [P, NB, D])
        AG = sb("AG", [P, NB * H])
        NW = sb("NW", [P, NB, H])
        NV = sb("NV", [P, NB, H])
        TB = sb("TB", [P, NB * (D + 1)])
        SK = sb("SK", [P, NB, D])
        st = sb("st", [P, 8, NB])
        SUM, VAR, BDEG, DDEG, BINV, DINV, SCL, TMP = range(8)

        ident = sb("ident", [P, P])
        lower = sb("lower", [P, P])
        ones_row = sb("ones_row", [1, P])
        w1 = sb("w1", [D, D])
        w2 = sb("w2", [D, D])
        we1 = sb("we1", [D, 3, H])
        we2 = sb("we2", [H, D])
        wn1 = sb("wn1", [D, 2, H])
        wn2 = sb("wn2", [H, D])
        wks = sb("wks", [D, H])
        wqv = sb("wqv", [D, H])
        brow = sb("brow", [1, 8, H])
        B1, B2, BE1, BN1, BN2, BKS, BQV = range(7)
        be2b = sb("be2b", [P, D])
        epsc = sb("epsc", [P, 2])
        xG = sb("xG", [P, 2, GROUP * H])
        xT = sb("xT", [P, 2, GROUP * P])

        isrc = sb("isrc", [EP, ET], i32)
        idst = sb("idst", [EP, ET], i32)
        gcol = sb("gcol", [EP, 2], i32)
        scol = sb("scol", [EP, 1])
        slot = sb("slot", [EP, 1])
        sidx = sb("sidx", [EP, 1], i32)
        rowid = sb("rowid", [EP, 1])
        dup = sb("dup", [EP, 2])
        eq = sb("eq", [EP, EP])
        eqlow = sb("eqlow", [EP, EP])
        msg = sb("msg", [EP, H + 1])
        msg2 = sb("msg2", [EP, H])
        tot = sb("tot", [EP, H + 1])
        ft = sb("ft", [EP, D])
        ftT = sb("ftT", [D, EP])
        mark = sb("mark", [1, 8])
        zero = sb("zero", [P, H + 1])

        PS = ctx.enter_context(nc.psum_tensor("PS", [P, 8 * 512], f32))

        weights_in = sem("weights_in")
        edges_in = sem("edges_in")
        x_in = sem("x_in")
        pool_const = sem("pool_const")
        dve_step = sem("dve_step")
        tab_ready = [sem(f"tab_ready{k}") for k in range(7)]
        tab_stored = [sem(f"tab_stored{k}") for k in range(7)]
        agg_in = [sem(f"agg_in{k}") for k in range(7)]
        lin_in = sem("lin_in")
        xG_in = sem("xG_in")
        xT_made = sem("xT_made")
        xT_copied = sem("xT_copied")
        lin_made = sem("lin_made")
        lin_kept = sem("lin_kept")
        std_in = sem("std_in")
        std_out = sem("std_out")
        out_ready = sem("out_ready")
        out_stored = sem("out_stored")
        cols = [sem(f"cols{k}") for k in range(7)]
        gathered = [sem(f"gathered{k}") for k in range(7)]
        sT_made = [sem(f"sT_made{k}") for k in range(7)]
        eq_made = [sem(f"eq_made{k}") for k in range(7)]
        tot_made = [sem(f"tot_made{k}") for k in range(7)]
        tot_ready = [sem(f"tot_ready{k}") for k in range(7)]
        added = [sem(f"added{k}") for k in range(7)]
        tile_done = [sem(f"tile_done{k}") for k in range(7)]
        zeroed = sem("zeroed")
        vec = [sem(f"vec{k}") for k in range(7)]
        ft_in = sem("ft_in")
        ftT_made = sem("ftT_made")
        ftT_kept = sem("ftT_kept")
        fe_made = sem("fe_made")
        gate_in = sem("gate_in")
        gate_out = sem("gate_out")

        block = ctx.enter_context(nc.Block())

        WEIGHTS = 16 * 20
        LIN = {
            "l0a": ([("NW", w1, D)], B1, D),
            "l0b": ([("NW", w2, D)], B2, D),
            "l1p": ([("XR", we1[:, 1, :], D)], BE1, H),
            "l1q": ([("XR", we1[:, 2, :], D)], None, H),
            "l1s": ([("AG", we2, H)], None, D),
            "l1h": ([("NW", wn1[:, 0, :], D), ("XR", wn1[:, 1, :], D)], BN1, H),
            "l1o": ([("NV", wn2, H)], BN2, D),
            "l2k": ([("XR", wks, D)], BKS, H),
            "l2q": ([("XR", wqv, D)], BQV, H),
        }
        ORDER = list(LIN)
        arrays = {"NW": NW, "XR": XR, "NV": NV}
        made = {}
        count = 0
        for name in ORDER:
            made[name] = count
            count += STEPS * len(LIN[name][0])

        def columns(which, i, w):
            if which == "AG":
                return AG[:, bass.ds(i * (GROUP * H), GROUP * H)].rearrange("p (b f) -> p b f", b=GROUP)
            return arrays[which][:, bass.ds(i * GROUP, GROUP), 0:w]

        BY_DST = [True, False, True, False, True, True, False]
        nodes = lambda ap: ap.rearrange("(p b) f -> p (b f)", p=P)

        @block.sync
        def _(sp):
            n = 0
            with nc.allow_non_contiguous_dma(reason="small weights"):
                for to, of in ((w1[:, :], W1), (w2[:, :], W2), (we1[:, :, :], We1.rearrange("(c d) h -> d c h", c=3)),
                               (we2[:, :], We2), (wn1[:, :, :], Wn1.rearrange("(c d) h -> d c h", c=2)),
                               (wn2[:, :], Wn2), (wks[:, 0:D], Wk), (wks[:, D:H], Ws),
                               (wqv[:, 0:D], Wq), (wqv[:, D:H], Wv)):
                    sp.dma_start(to, of).then_inc(weights_in, 16)
                    n += 16
                for row, c0, of in ((B1, 0, b1), (B2, 0, b2), (BE1, 0, be1), (BN1, 0, bn1), (BN2, 0, bn2),
                                    (BKS, 0, bk), (BKS, D, bs), (BQV, 0, bq), (BQV, D, bv)):
                    w = of.shape[0]
                    sp.dma_start(brow[0:1, row, c0:c0 + w], of.rearrange("(a n) -> a n", a=1)).then_inc(weights_in, 16)
                    n += 16
                sp.dma_start(be2b[:, :], be2.rearrange("(a n) -> a n", a=1).to_broadcast((P, D))).then_inc(weights_in, 16)
                n += 16
            assert n == WEIGHTS
            sp.dma_start(isrc[:, :], src.rearrange("(p t) -> p t", p=EP)).then_inc(edges_in, 16)
            sp.dma_start(idst[:, :], dst.rearrange("(p t) -> p t", p=EP)).then_inc(edges_in, 16)
            sp.wait_ge(pool_const, 2)
            sp.dma_start(XR[0:FULL, :, :], x[0:FULL * NB, :].rearrange("(p b) f -> p b f", p=FULL)).then_inc(x_in, 16)
            sp.dma_start(XR[FULL:FULL + 1, 0:REST, :],
                         x[FULL * NB:N, :].rearrange("(p b) f -> p b f", p=1)).then_inc(x_in, 16)
            for k in range(7):
                w = W_TAB[k]
                z = acc[k].rearrange("(r p) f -> p r f", p=P)
                sp.dma_start(z, zero[:, 0:w].rearrange("p (a w) -> p a w", a=1).to_broadcast((P, NB + 1, w)))\
                    .then_inc(zeroed, 16)
            for k in range(7):
                w = W_TAB[k]
                sp.wait_ge(tab_ready[k], 1)
                if k < 2:
                    sp.dma_start(nodes(tab[k]), TB[:, :]).then_inc(tab_stored[k], 16)
                elif k == 4:
                    sp.dma_start(nodes(tab[4]), NW[:, :, :].rearrange("p b f -> p (b f)")).then_inc(tab_stored[k], 16)
                    sp.dma_start(nodes(tab_src[4]), NV[:, :, :].rearrange("p b f -> p (b f)")).then_inc(tab_stored[k], 16)
                elif k == 5:
                    sp.dma_start(tab[5].rearrange("(p b) f -> p b f", p=P), NW[:, :, 0:D]).then_inc(tab_stored[k], 16)
                    sp.dma_start(nodes(tab_src[5]), NV[:, :, :].rearrange("p b f -> p (b f)")).then_inc(tab_stored[k], 16)
                else:
                    sp.dma_start(tab[k].rearrange("(p b) f -> p b f", p=P), NW[:, :, 0:D]).then_inc(tab_stored[k], 16)
                if k == 4:
                    ftv = feat.rearrange("(p t) f -> p t f", p=EP)
                    with sp.Fori(0, ET) as t:
                        sp.wait_ge(tile_done[4], t + 1)
                        sp.dma_start(ft[:, :], ftv[:, bass.ts(t, 1), :].rearrange("p a f -> p (a f)")).then_inc(ft_in, 16)
                sp.wait_ge(added[k], 16 * ET)
                sp.dma_start(AG[:, 0:NB * w], nodes(acc[k][0:NP, :])).then_inc(agg_in[k], 16)
            sp.wait_ge(out_ready, 1)
            sp.dma_start(out[0:FULL * NB, :].rearrange("(p b) f -> p b f", p=FULL), XR[0:FULL, :, :]).then_inc(out_stored, 16)
            sp.dma_start(out[FULL * NB:N, :].rearrange("(p b) f -> p b f", p=1),
                         XR[FULL:FULL + 1, 0:REST, :]).then_inc(out_stored, 16)
            sp.wait_ge(out_stored, 32)

        @block.gpsimd
        def _(pool):
            pool.memset(zero[:, :], 0.0).then_inc(pool_const, 1)
            pool.memset(XR[:, :, :], 0.0).then_inc(pool_const, 1)
            pool.memset(ident[:, :], 0.0).then_inc(pool_const, 1)
            pool.memset(lower[:, :], 0.0).then_inc(pool_const, 1)
            pool.memset(ones_row[:, :], 1.0).then_inc(pool_const, 1)
            pool.memset(epsc[:, 0:1], EPS).then_inc(pool_const, 1)
            pool.memset(epsc[:, 1:2], DEG_EPS).then_inc(pool_const, 1)
            pool.wait_ge(pool_const, 4)
            pool.affine_select(out=ident[:, :], in_=ident[:, :], compare_op=ALU.not_equal, fill=1.0,
                               base=0, pattern=[[-1, P]], channel_multiplier=1).then_inc(pool_const, 1)
            pool.affine_select(out=lower[:, :], in_=lower[:, :], compare_op=ALU.is_ge, fill=1.0,
                               base=0, pattern=[[1, P]], channel_multiplier=-1).then_inc(pool_const, 1)
            pool.iota(rowid[:, :], pattern=[[0, 1]], base=NP, channel_multiplier=1,
                      allow_small_or_imprecise_dtypes=True).then_inc(pool_const, 1)

            def linear(name):
                terms, bias, wo = LIN[name]
                pool.wait_ge(lin_in, ORDER.index(name) + 1)
                with pool.Fori(0, STEPS) as i:
                    for a, (which, wt, wi) in enumerate(terms):
                        pool.wait_ge(xT_made, i * len(terms) + (made[name] + 1))
                        pool.tensor_copy(xG[:, a, 0:GROUP * wi].rearrange("p (b f) -> p b f", b=GROUP),
                                         columns(which, i, wi)).then_inc(xG_in, 1)

            BEFORE = {2: ["l0a"], 4: ["l0b", "l1p", "l1q"], 5: ["l1s", "l1h", "l1o", "l2k", "l2q"]}
            for k in range(7):
                w = W_TAB[k]
                for name in BEFORE.get(k, []):
                    linear(name)
                pool.wait_ge(tab_stored[k], 32 if k in (4, 5) else 16)
                idx = lambda c: bass.IndirectOffsetOnAxis(ap=gcol[:, c:c + 1].bitcast(u32), axis=0)
                pool.wait_ge(zeroed, 16 * 7)
                pool.memset(mark[:, k:k + 1], 0.0).then_inc(tile_done[k], 1)
                with pool.Fori(0, ET) as t:
                    pool.wait_ge(cols[k], t + 1)
                    pool.nop(nofuse=True)
                    if k in (4, 5):
                        pool.indirect_dma_start(msg[:, 0:w], None, tab[k], idx(0)).then_inc(gathered[k], 16)
                        pool.indirect_dma_start(msg2[:, 0:H], None, tab_src[k], idx(1)).then_inc(gathered[k], 16)
                    else:
                        pool.indirect_dma_start(msg[:, 0:w], None, tab[k], idx(1 if BY_DST[k] else 0))\
                            .then_inc(gathered[k], 16)
                    pool.wait_ge(tot_ready[k], t + 1)
                    pool.nop(nofuse=True)
                    pool.indirect_dma_start(acc[k], bass.IndirectOffsetOnAxis(ap=sidx[:, 0:1].bitcast(u32), axis=0),
                                            tot[:, 0:w], None, compute_op=ALU.add).then_inc(added[k], 16)
                    pool.wait_ge(added[k], 16 * t + 16)
                    pool.nop(nofuse=True)
                    pool.memset(mark[:, k:k + 1], 0.0).then_inc(tile_done[k], 1)

        @block.tensor
        def _(pe):
            pe.wait_ge(pool_const, 10)
            pe.wait_ge(weights_in, WEIGHTS)

            def linear(name):
                terms, bias, wo = LIN[name]
                at = ORDER.index(name)
                with pe.Fori(0, STEPS) as i:
                    for a, (which, wt, wi) in enumerate(terms):
                        pe.wait_ge(xT_copied, i * len(terms) + made[name] + a + 1)
                        pe.wait_ge(xG_in, i * len(terms) + made[name] + a + 1)
                        for j in range(GROUP):
                            last = nc.tensor.matmul(PS[0:wi, a * 1024 + j * P:a * 1024 + (j + 1) * P],
                                                    xG[:, a, j * wi:(j + 1) * wi], ident[:, :], start=True, stop=True)
                        last.then_inc(xT_made, 1)
                    pe.wait_ge(xT_copied, (i + 1) * len(terms) + made[name] + 1)
                    pe.wait_ge(lin_kept, i + (at * STEPS + 1))
                    for j in range(GROUP):
                        o = PS[:, 2048 + j * wo:2048 + (j + 1) * wo]
                        for a, (which, wt, wi) in enumerate(terms):
                            last = nc.tensor.matmul(o, xT[0:wi, a, j * P:(j + 1) * P], wt[:, :] if wt is not None else None,
                                                    start=a == 0, stop=bias is None and a == len(terms) - 1)
                        if bias is not None:
                            last = nc.tensor.matmul(o, ones_row[0:1, :], brow[0:1, bias, 0:wo], start=False, stop=True)
                    last.then_inc(lin_made, 1)

            def edge_pass(k):
                w = W_TAB[k]
                with pe.Fori(0, ET) as t:
                    pe.wait_ge(cols[k], t + 1)
                    nc.tensor.matmul(PS[0:EP, 0:EP], scol[:, 0:1].to_broadcast((EP, EP)), ident[0:EP, 0:EP],
                                     start=True, stop=True).then_inc(sT_made[k], 1)
                    if k == 4:
                        pe.wait_ge(ft_in, 16 * t + 16)
                        nc.tensor.matmul(PS[0:D, 1024:1024 + EP], ft[:, :], ident[0:EP, 0:EP], start=True, stop=True)\
                            .then_inc(ftT_made, 1)
                        pe.wait_ge(ftT_kept, t + 1)
                        nc.tensor.matmul(PS[0:EP, 1536:1536 + H], ftT[:, :], we1[:, 0, :], start=True, stop=True)\
                            .then_inc(fe_made, 1)
                    pe.wait_ge(eq_made[k], t + 1)
                    nc.tensor.matmul(PS[0:EP, 512:512 + w], eq[:, :], msg[:, 0:w], start=True, stop=True)\
                        .then_inc(tot_made[k], 1)

            edge_pass(0)
            edge_pass(1)
            linear("l0a")
            edge_pass(2)
            edge_pass(3)
            linear("l0b")
            linear("l1p")
            linear("l1q")
            edge_pass(4)
            linear("l1s")
            linear("l1h")
            linear("l1o")
            linear("l2k")
            linear("l2q")
            edge_pass(5)
            edge_pass(6)

        @block.scalar
        def _(act):
            act.wait_ge(pool_const, 7)
            nc.scalar.activation(epsc[0:1, 0:1], epsc[0:1, 0:1], ACT.Copy).then_inc(xT_copied, 1)

            def linear(name):
                terms, bias, wo = LIN[name]
                with act.Fori(0, STEPS) as i:
                    for a, (which, wt, wi) in enumerate(terms):
                        act.wait_ge(xT_made, i * len(terms) + (made[name] + a + 2))
                        nc.scalar.activation(xT[0:wi, a, :], PS[0:wi, a * 1024:a * 1024 + GROUP * P], ACT.Copy)\
                            .then_inc(xT_copied, 1)

            def norm(n):
                act.wait_ge(std_in, n + 1)
                nc.scalar.activation(st[:, TMP, :], st[:, VAR, :], ACT.Sqrt, bias=epsc[:, 0:1], scale=1.0 / D)\
                    .then_inc(std_out, 1)

            def gates():
                with act.Fori(0, ET) as t:
                    act.wait_ge(gate_in, t + 1)
                    nc.scalar.activation(msg[:, 0:D], msg[:, 0:D], ACT.Sigmoid).then_inc(gate_out, 1)

            linear("l0a")
            linear("l0b")
            norm(0)
            linear("l1p")
            linear("l1q")
            linear("l1s")
            linear("l1h")
            linear("l1o")
            norm(1)
            linear("l2k")
            linear("l2q")
            gates()
            norm(2)
            act.wait_ge(std_in, 4)
            nc.scalar.activation(st[:, TMP, :], st[:, SUM, :], ACT.Sqrt, bias=epsc[:, 1:2]).then_inc(std_out, 1)
            norm(4)

        @block.vector
        def _(dve):
            done = [0]

            def step(ins):
                done[0] += 1
                ins.then_inc(dve_step, 1)
                dve.wait_ge(dve_step, done[0])

            V = nc.vector
            step(V.memset(st[:, :, :], 0.0))
            V.memset(gcol[:, :], 0).then_inc(xT_made, 1)
            V.memset(TB[:, :], 1.0).then_inc(lin_kept, 1)

            def per_node(row, w):
                return st[:, row, :].rearrange("p (b a) -> p b a", a=1).to_broadcast((P, NB, w))

            def keep(name, to, relu=False):
                terms, bias, wo = LIN[name]
                at = ORDER.index(name)
                with dve.Fori(0, STEPS) as i:
                    dve.wait_ge(lin_made, i + (at * STEPS + 1))
                    o = PS[:, 2048:2048 + GROUP * wo].rearrange("p (b f) -> p b f", b=GROUP)
                    t = to[:, bass.ds(i * GROUP, GROUP), 0:wo]
                    V.tensor_scalar(t, o, 0.0 if relu else 1.0, None, ALU.max if relu else ALU.mult).then_inc(lin_kept, 1)
                dve.wait_ge(lin_kept, (at + 1) * STEPS + 1)

            norms = [0]

            def root():
                norms[0] += 1
                dve.wait_ge(std_out, norms[0])

            def layer_norm():
                step(V.tensor_reduce(st[:, SUM, :], XR[:, :, :], AX.X, ALU.add))
                step(V.tensor_scalar(st[:, SUM, :], st[:, SUM, :], 1.0 / D, None, ALU.mult))
                step(V.tensor_tensor(XR[:, :, :], XR[:, :, :], per_node(SUM, D), ALU.subtract))
                step(V.tensor_tensor(NV[:, :, 0:D], XR[:, :, :], XR[:, :, :], ALU.mult))
                V.tensor_reduce(st[:, VAR, :], NV[:, :, 0:D], AX.X, ALU.add).then_inc(std_in, 1)
                root()
                step(V.reciprocal(st[:, TMP, :], st[:, TMP, :]))
                step(V.tensor_tensor(XR[:, :, :], XR[:, :, :], per_node(TMP, D), ALU.mult))

            def inverse(to, of):
                step(V.tensor_scalar(st[:, TMP, :], st[:, of, :], 1.0, None, ALU.max))
                step(V.reciprocal(st[:, TMP, :], st[:, TMP, :]))
                step(V.tensor_scalar(st[:, to, :], st[:, of, :], 0.0, None, ALU.is_gt))
                step(V.tensor_tensor(st[:, to, :], st[:, to, :], st[:, TMP, :], ALU.mult))

            def edge_pass(k):
                w = W_TAB[k]
                steps = {4: 7, 5: 5}.get(k, 4)
                by, other = (idst, isrc) if BY_DST[k] else (isrc, idst)
                with dve.Fori(0, ET) as t:
                    n = [0]

                    def own(ins):
                        n[0] += 1
                        ins.then_inc(vec[k], 1)
                        dve.wait_ge(vec[k], t * steps + n[0])

                    dve.wait_ge(tile_done[k], t + 1)
                    V.tensor_copy(gcol[:, 0:1], idst[:, bass.ts(t, 1)])
                    V.tensor_copy(gcol[:, 1:2], isrc[:, bass.ts(t, 1)])
                    own(V.tensor_copy(scol[:, :], by[:, bass.ts(t, 1)]))
                    V.tensor_scalar(slot[:, :], scol[:, :], -1.0, rowid[:, :], ALU.mult, ALU.add).then_inc(cols[k], 1)
                    dve.wait_ge(sT_made[k], t + 1)
                    own(V.tensor_scalar(eq[:, :], PS[0:EP, 0:EP], scol[:, 0:1], None, ALU.is_equal))
                    own(V.tensor_tensor(eqlow[:, :], eq[:, :], lower[0:EP, 0:EP], ALU.mult))
                    own(V.tensor_reduce(dup[:, 0:1], eqlow[:, :], AX.X, ALU.max))
                    if k == 4:
                        dve.wait_ge(ftT_made, t + 1)
                        V.tensor_copy(ftT[:, :], PS[0:D, 1024:1024 + EP]).then_inc(ftT_kept, 1)
                        dve.wait_ge(gathered[k], 32 * t + 32)
                        own(V.tensor_tensor(msg[:, 0:H], msg[:, 0:H], msg2[:, :], ALU.add))
                        dve.wait_ge(fe_made, t + 1)
                        own(V.tensor_tensor(msg[:, 0:H], msg[:, 0:H], PS[0:EP, 1536:1536 + H], ALU.add))
                        own(V.tensor_scalar(msg[:, 0:H], msg[:, 0:H], 0.0, None, ALU.max))
                    elif k == 5:
                        dve.wait_ge(gathered[k], 32 * t + 32)
                        V.tensor_tensor(msg[:, 0:D], msg[:, 0:D], msg2[:, 0:D], ALU.add).then_inc(gate_in, 1)
                        dve.wait_ge(gate_out, t + 1)
                        own(V.tensor_tensor(msg[:, 0:D], msg[:, 0:D], msg2[:, D:H], ALU.mult))
                    else:
                        dve.wait_ge(gathered[k], 16 * t + 16)
                    V.scalar_tensor_tensor(sidx[:, :], dup[:, 0:1], slot[:, 0:1], scol[:, :], ALU.mult, ALU.add)\
                        .then_inc(eq_made[k], 1)
                    dve.wait_ge(tot_made[k], t + 1)
                    V.tensor_copy(tot[:, 0:w], PS[0:EP, 512:512 + w]).then_inc(tot_ready[k], 1)

            TB3 = TB[:, :].rearrange("p (b f) -> p b f", b=NB)

            def sums(w):
                return AG[:, 0:NB * w].rearrange("p (b f) -> p b f", b=NB)

            dve.wait_ge(pool_const, 10)
            dve.wait_ge(edges_in, 32)
            dve.wait_ge(x_in, 32)
            dve.wait_ge(weights_in, WEIGHTS)

            dve.wait_ge(lin_kept, 1)
            V.tensor_copy(TB3[:, :, 0:D], XR[:, :, :]).then_inc(tab_ready[0], 1)
            edge_pass(0)
            dve.wait_ge(agg_in[0], 16)
            step(V.tensor_copy(st[:, BDEG, :], sums(D + 1)[:, :, D:D + 1].rearrange("p b a -> p (b a)")))
            inverse(BINV, BDEG)
            dve.wait_ge(tab_stored[0], 16)
            V.tensor_tensor(TB3[:, :, 0:D], sums(D + 1)[:, :, 0:D], per_node(BINV, D), ALU.mult).then_inc(tab_ready[1], 1)
            edge_pass(1)
            dve.wait_ge(agg_in[1], 16)
            step(V.tensor_copy(st[:, DDEG, :], sums(D + 1)[:, :, D:D + 1].rearrange("p b a -> p (b a)")))
            inverse(DINV, DDEG)
            V.tensor_tensor(NW[:, :, 0:D], sums(D + 1)[:, :, 0:D], per_node(DINV, D), ALU.mult).then_inc(lin_in, 1)
            keep("l0a", NW, relu=True)
            V.tensor_scalar(NW[:, :, 0:D], NW[:, :, 0:D], 1.0, None, ALU.mult).then_inc(tab_ready[2], 1)
            edge_pass(2)
            dve.wait_ge(agg_in[2], 16)
            V.tensor_tensor(NW[:, :, 0:D], sums(D), per_node(BINV, D), ALU.mult).then_inc(tab_ready[3], 1)
            edge_pass(3)
            dve.wait_ge(agg_in[3], 16)
            V.tensor_tensor(NW[:, :, 0:D], sums(D), per_node(DINV, D), ALU.mult).then_inc(lin_in, 1)
            keep("l0b", NW)
            step(V.tensor_tensor(XR[:, :, :], XR[:, :, :], NW[:, :, 0:D], ALU.add))
            layer_norm()

            V.memset(st[:, SUM, :], 0.0).then_inc(lin_in, 2)
            keep("l1p", NW)
            keep("l1q", NV)
            V.memset(st[:, SUM, :], 0.0).then_inc(tab_ready[4], 1)
            edge_pass(4)
            dve.wait_ge(agg_in[4], 16)
            V.memset(st[:, VAR, :], 0.0).then_inc(lin_in, 1)
            keep("l1s", NW)
            step(V.tensor_tensor(NV[:, :, 0:D], per_node(BDEG, D),
                                 be2b[:, :].rearrange("p (a f) -> p a f", a=1).to_broadcast((P, NB, D)), ALU.mult))
            V.tensor_tensor(NW[:, :, 0:D], NW[:, :, 0:D], NV[:, :, 0:D], ALU.add).then_inc(lin_in, 1)
            keep("l1h", NV, relu=True)
            V.memset(st[:, VAR, :], 0.0).then_inc(lin_in, 1)
            keep("l1o", NW)
            step(V.tensor_tensor(XR[:, :, :], XR[:, :, :], NW[:, :, 0:D], ALU.add))
            layer_norm()

            V.memset(st[:, SUM, :], 0.0).then_inc(lin_in, 2)
            keep("l2k", NW)
            keep("l2q", NV)
            step(V.tensor_copy(SK[:, :, :], NW[:, :, D:H]))
            V.memset(st[:, SUM, :], 0.0).then_inc(tab_ready[5], 1)
            edge_pass(5)
            dve.wait_ge(agg_in[5], 16)
            step(V.tensor_tensor(XR[:, :, :], XR[:, :, :], sums(D), ALU.add))
            step(V.tensor_tensor(XR[:, :, :], XR[:, :, :], SK[:, :, :], ALU.add))
            layer_norm()

            step(V.tensor_scalar(st[:, DDEG, :], st[:, DDEG, :], 1.0, None, ALU.add))
            step(V.tensor_scalar(st[:, DINV, :], st[:, DDEG, :], DEG_EPS, None, ALU.add))
            step(V.reciprocal(st[:, DINV, :], st[:, DINV, :]))
            V.tensor_tensor(st[:, SUM, :], st[:, DDEG, :], st[:, DINV, :], ALU.mult).then_inc(std_in, 1)
            root()
            step(V.reciprocal(st[:, SCL, :], st[:, TMP, :]))
            step(V.tensor_tensor(SK[:, :, :], XR[:, :, :], per_node(SCL, D), ALU.mult))
            V.tensor_copy(NW[:, :, 0:D], SK[:, :, :]).then_inc(tab_ready[6], 1)
            step(V.tensor_tensor(st[:, SCL, :], st[:, SCL, :], st[:, DINV, :], ALU.mult))
            edge_pass(6)
            dve.wait_ge(agg_in[6], 16)
            step(V.tensor_tensor(SK[:, :, :], SK[:, :, :], sums(D), ALU.add))
            step(V.tensor_tensor(SK[:, :, :], SK[:, :, :], per_node(SCL, D), ALU.mult))
            step(V.tensor_tensor(XR[:, :, :], XR[:, :, :], SK[:, :, :], ALU.add))
            layer_norm()
            V.memset(st[:, SUM, :], 0.0).then_inc(out_ready, 1)


_INS = ['x', 'src', 'dst', 'edge_attr_64', 'L0_gnn_W1', 'L0_gnn_b1', 'L0_gnn_W2', 'L0_gnn_b2',
        'L1_gnn_We1', 'L1_gnn_be1', 'L1_gnn_We2', 'L1_gnn_be2', 'L1_gnn_Wn1', 'L1_gnn_bn1', 'L1_gnn_Wn2', 'L1_gnn_bn2',
        'L2_gnn_W_key', 'L2_gnn_b_key', 'L2_gnn_W_query', 'L2_gnn_b_query', 'L2_gnn_W_value', 'L2_gnn_b_value',
        'L2_gnn_W_skip', 'L2_gnn_b_skip']
_OUTS = [((N, D), 'float32')]


def kernel(**inputs):
    import numpy as _np
    import concourse.bacc as _bacc
    from concourse import mybir as _mybir
    from concourse.bass_utils import run_bass_kernel_spmd as _run

    nc = _bacc.Bacc("TRN2", target_bir_lowering=False, num_devices=1)
    arrays, args = {}, []
    for name in _INS:
        a = _np.ascontiguousarray(inputs[name])
        arrays[f"in_{name}_dram"] = a
        args.append(nc.dram_tensor(f"in_{name}_dram", a.shape, _mybir.dt.from_np(a.dtype), kind="ExternalInput").ap())
    for i, (shape, dtype) in enumerate(_OUTS):
        dt = _mybir.dt.from_np(_np.dtype(dtype))
        args.append(nc.dram_tensor(f"out_{i}_dram", shape, dt, kind="ExternalOutput").ap())
    build(nc, *args)
    r = _run(nc, [arrays], core_ids=[0])
    return r.results[0]["out_0_dram"]
```

```python
import concourse.bass as bass
from concourse import mybir
from contextlib import ExitStack


N = 6250
E = 206250
D = 64
H = 128
P = 128
NB = -(-N // P)
NP = NB * P
FULL = N // NB
REST = N - FULL * NB
GROUP = 7
STEPS = NB // GROUP
EP = 125
ET = E // EP
WT = 36
WE = WT * P
SLOTS = P
FROWS = NB * NB * SLOTS
CH = 7
NC = NB // CH
EPS = 1e-5
DEG_EPS = 1e-8


def build(nc, x, src, dst, feat, W1, b1, W2, b2, We1, be1, We2, be2, Wn1, bn1, Wn2, bn2,
          Wk, bk, Wq, bq, Wv, bv, Ws, bs, out):
    f32 = mybir.dt.float32
    i32 = mybir.dt.int32
    u32 = mybir.dt.uint32
    bf16 = mybir.dt.bfloat16
    ARENA = 147 * 1024
    ALU = mybir.AluOpType
    ACT = mybir.ActivationFunctionType
    AX = mybir.AxisListType

    ctx = ExitStack()
    with ctx:
        def sb(name, shape, dt=f32):
            return ctx.enter_context(nc.sbuf_tensor(name, shape, dt))

        def sem(name):
            return ctx.enter_context(nc.semaphore(name))

        W_TAB = [D + 1, D + 1, D, D, H, D, D]
        tab = [nc.dram_tensor(f"tab{k}", (NP, w), f32, kind="Internal").ap()
               for k, w in enumerate([D + 1, D + 1, D, D, H, D, D])]
        tab_src = {4: nc.dram_tensor("tab_l1_src", (NP, H), f32, kind="Internal").ap(),
                   5: nc.dram_tensor("tab_l2_src", (NP, H), f32, kind="Internal").ap()}
        acc = [nc.dram_tensor(f"acc{k}", (NP + P, w), f32, kind="Internal").ap() for k, w in enumerate(W_TAB)]

        cnt_t = nc.dram_tensor("cnt_t", (NB, P, NB * P), bf16, kind="Internal").ap()
        cnt_s = nc.dram_tensor("cnt_s", (NB, P, NB * P), bf16, kind="Internal").ap()
        feat_slot = nc.dram_tensor("feat_slot", (FROWS, D), f32, kind="Internal").ap()
        slot_rows = nc.dram_tensor("slot_rows", (NB, 2 * NB, P), bf16, kind="Internal").ap()

        arena = sb("arena", [P, ARENA // 4])
        taken = {}

        def carve(kb, n, dt=f32, parts=P):
            a = int(kb * 256)
            size = {f32: 4, i32: 4, bf16: 2}[dt] * n
            b = a + -(-size // 4)
            assert b * 4 <= ARENA, (kb, n)
            v = arena[0:parts, a:b]
            return v if dt is f32 else v.bitcast(dt)[:, 0:n]

        XR = sb("XR", [P, NB, D])
        AG = carve(26, NB * H)
        NW = carve(51, NB * H).rearrange("p (b f) -> p b f", b=NB)
        NV = carve(76, NB * H).rearrange("p (b f) -> p b f", b=NB)
        TB = carve(101, NB * (D + 1))
        SK = sb("SK", [P, NB, D])
        st = sb("st", [P, 8, NB])
        SUM, VAR, BDEG, DDEG, BINV, DINV, SCL, TMP = range(8)

        ident = sb("ident", [P, P])
        lower = sb("lower", [P, P])
        ones_row = sb("ones_row", [1, P])
        w1 = sb("w1", [D, D])
        w2 = sb("w2", [D, D])
        we1 = sb("we1", [D, 3, H])
        we2 = sb("we2", [H, D])
        wn1 = sb("wn1", [D, 2, H])
        wn2 = sb("wn2", [H, D])
        wks = sb("wks", [D, H])
        wqv = sb("wqv", [D, H])
        brow = sb("brow", [1, 8, H])
        B1, B2, BE1, BN1, BN2, BKS, BQV = range(7)
        be2b = sb("be2b", [P, D])
        epsc = sb("epsc", [P, 2])
        xG = carve(114, 2 * GROUP * H).rearrange("p (a n) -> p a n", a=2)
        xT = [carve(121 + 7 * i, 2 * GROUP * P).rearrange("p (a n) -> p a n", a=2) for i in range(2)]

        isrc = carve(26, ET, i32, EP)
        idst = carve(33, ET, i32, EP)
        gcol = sb("gcol", [EP, 2], i32)
        scol = sb("scol", [EP, 1])
        slot = sb("slot", [EP, 1])
        sidx = sb("sidx", [EP, 1], i32)
        rowid = sb("rowid", [EP, 1])
        dup = sb("dup", [EP, 2])
        eq = sb("eq", [EP, EP])
        eqlow = sb("eqlow", [EP, EP])
        msg = sb("msg", [EP, H + 1])
        msg2 = sb("msg2", [EP, H])
        tot = sb("tot", [EP, H + 1])
        ft = sb("ft", [EP, D])
        ftT = sb("ftT", [D, EP])
        mark = sb("mark", [1, 8])
        zero = sb("zero", [P, H + 1])

        iota1 = sb("iota1", [P, P], bf16)
        identb = sb("identb", [P, P], bf16)
        upperb = sb("upperb", [P, P], bf16)
        ones_col = sb("ones_col", [P, 1])
        wcol = sb("wcol", [P, NB])
        wfirst = sb("wfirst", [P, NB])
        wrow = sb("wrow", [P, NB])
        spare = sb("spare", [P, 1])
        cnt = sb("cnt", [P, NB])
        start_i = sb("start_i", [1, NB], i32)
        rank = sb("rank", [P, WT])
        fit = sb("fit", [P, 2, WT])
        srow = sb("srow", [P, 2, WT])
        placed = sb("placed", [P, NB])
        vmark = sb("vmark", [1, 1])
        placed1 = sb("placed1", [P, 1])
        flag_i = sb("flag_i", [1, 1], i32)
        SD = sb("SD", [P, NB * 2 * NB], bf16)
        sidx_p = [sb(f"sidx_p{h}", [P, WT], i32) for h in range(2)]
        sd1 = sb("sd1", [P, P], bf16)
        fwin = [carve(0, WT * D), carve(9, WT * D)]
        sidx_w = carve(18, NB * WT, i32)
        srcw = carve(26, NB * WT, i32)
        dstw = carve(33, NB * WT, i32)
        q_f = carve(40, NB * WT)
        r_f = carve(47, NB * WT)
        t_f = carve(54, NB * WT)
        q_i = carve(61, NB * WT, i32)
        class_b = carve(68, NB * WT, bf16)
        pay = carve(72, 2 * NB * WT, bf16).rearrange("p (k n) -> p k n", k=2)
        ohx = carve(79, NB * (WT + 1), bf16)
        ranks = carve(83, NB * (WT + 1), bf16)
        prod = carve(87, NB * WT, bf16)
        mask = carve(91, NB * (WT + 1), bf16)
        classes = carve(95, NB * WT, bf16)
        rowsT = carve(114, NB * P, bf16, 2 * NB)
        wpay = carve(127, WT * 2 * NB, bf16)
        ohr = carve(134, WT * P, bf16)
        blk = carve(95, ET, bf16, EP)
        prod_junk = carve(87, ET, bf16, EP)
        ohs_c = [carve(26 + 2 * c, CH * P, bf16) for c in range(NC)]
        oht_c = [carve(40 + 2 * c, CH * P, bf16) for c in range(NC)]
        ct_c = [carve(54 + 2 * c, CH * P, bf16) for c in range(NC)]
        cs_c = [carve(68 + 2 * c, CH * P, bf16) for c in range(NC)]
        ptab = carve(76, NB * (D + 1))
        pres = carve(89, NB * (D + 1))
        psplit = carve(114, NB * 3 * (D + 1), bf16)
        cring = [carve(134, CH * P, bf16)] + [carve(102 + 2 * c, CH * P, bf16) for c in range(6)]
        ysum = carve(51, NB * (D + 1))
        y0 = sb("y0", [P, H])
        ystage = sb("ystage", [P, H])
        pnum1 = sb("pnum1", [P, 1])
        qsplit = carve(0, NB * 3 * H, bf16)
        dsplit = carve(36.75, NB * 3 * H, bf16)
        dtab = carve(73.5, NB * H)
        qtab = carve(98, NB * H)
        selS = [carve(73.5 + 1.75 * c, CH * P, bf16) for c in range(NC)]
        selT = [carve(85.75 + 1.75 * c, CH * P, bf16) for c in range(NC)]
        sumT = [carve(98 + 1.75 * c, CH * P, bf16) for c in range(NC)]
        fslot = [carve(110.25 + 1.75 * c, CH * D) for c in range(NC)]
        hid = [carve(122.5 + 8.75 * i, CH * P) for i in range(2)]
        parts3 = [carve(126 + 8.75 * i, 3 * CH * P, bf16) for i in range(2)]
        fT = [carve(140 + 3.5 * i, CH * P)[0:D, :] for i in range(2)]

        PS = ctx.enter_context(nc.psum_tensor("PS", [P, 8 * 512], f32))

        weights_in = sem("weights_in")
        edges_in = sem("edges_in")
        edges2_in = [sem(f"edges2_in{k}") for k in range(7)]
        x_in = sem("x_in")
        pool_const = sem("pool_const")
        dve_step = sem("dve_step")
        tab_ready = sem("tab_ready")
        tab_stored = [sem(f"tab_stored{k}") for k in range(7)]
        agg_in = [sem(f"agg_in{k}") for k in range(7)]
        lin_in = sem("lin_in")
        xG_in = sem("xG_in")
        xT_made = sem("xT_made")
        xT_copied = sem("xT_copied")
        lin_made = sem("lin_made")
        lin_kept = sem("lin_kept")
        std_in = sem("std_in")
        std_out = sem("std_out")
        out_ready = sem("out_ready")
        out_stored = sem("out_stored")
        const_ready = sem("const_ready")
        counted = sem("counted")
        start_made = sem("start_made")
        start_ready = sem("start_ready")
        window_in = sem("window_in")
        slot_step = sem("slot_step")
        oh_made = sem("oh_made")
        before_made = sem("before_made")
        before_kept = sem("before_kept")
        ohr_made = sem("ohr_made")
        slots_made = sem("slots_made")
        sd_kept = sem("sd_kept")
        rows_made = sem("rows_made")
        rows_kept = sem("rows_kept")
        rows_stored = sem("rows_stored")
        srow_made = sem("srow_made")
        sidx_kept = sem("sidx_kept")
        filled = [sem(f"filled{i}") for i in range(2)]
        fwin_in = [sem(f"fwin_in{i}") for i in range(2)]
        feat_put = [sem(f"feat_put{i}") for i in range(2)]
        placed_ready = sem("placed_ready")
        total_made = sem("total_made")
        flag_ready = sem("flag_ready")
        hot_made = sem("hot_made")
        cnt_made = sem("cnt_made")
        ct_kept = sem("ct_kept")
        cs_kept = sem("cs_kept")
        cnt_stored = [sem(f"cnt_stored{c}") for c in range(NC)]
        ptab_in = sem("ptab_in")
        hi_made = sem("hi_made")
        res_made = sem("res_made")
        mid_made = sem("mid_made")
        split_made = sem("split_made")
        ring_in = [sem(f"ring_in{c}") for c in range(NC)]
        ring_used = sem("ring_used")
        ya_made = sem("ya_made")
        ya_kept = sem("ya_kept")
        yb_made = sem("yb_made")
        yb_kept = sem("yb_kept")
        agg_kept = sem("agg_kept")
        y_all = sem("y_all")
        y_stored = sem("y_stored")
        splits_hi = sem("splits_hi")
        splits_res = sem("splits_res")
        splits_mid = sem("splits_mid")
        splits_lo = sem("splits_lo")
        tabs_in = [sem(f"tabs_in{i}") for i in range(2)]
        slot_in = [sem(f"slot_in{c}") for c in range(NC)]
        sel_made = sem("sel_made")
        fT_made = sem("fT_made")
        fT_kept = sem("fT_kept")
        pre_made = sem("pre_made")
        pre_free = sem("pre_free")
        gate_made = sem("gate_made")
        msg_made = sem("msg_made")
        msg_hi = sem("msg_hi")
        msg_res = sem("msg_res")
        msg_mid = sem("msg_mid")
        msg_lo = sem("msg_lo")
        agg_made = sem("agg_made")
        za_kept = sem("za_kept")
        zb_kept = sem("zb_kept")
        cols = sem("cols")
        gathered = [sem(f"gathered{k}") for k in range(7)]
        sT_made = sem("sT_made")
        eq_made = sem("eq_made")
        tot_made = sem("tot_made")
        tot_ready = sem("tot_ready")
        added = [sem(f"added{k}") for k in range(7)]
        tile_done = sem("tile_done")
        zeroed = [sem(f"zeroed{k}") for k in range(7)]
        vec = sem("vec")
        ft_in = sem("ft_in")
        ftT_made = sem("ftT_made")
        ftT_kept = sem("ftT_kept")
        fe_made = sem("fe_made")
        gate_in = sem("gate_in")
        gate_out = sem("gate_out")

        block = ctx.enter_context(nc.Block())

        WEIGHTS = 16 * 20
        LIN = {
            "l0a": ([("NW", w1, D)], B1, D),
            "l0b": ([("NW", w2, D)], B2, D),
            "l1p": ([("XR", we1[:, 1, :], D)], BE1, H),
            "l1q": ([("XR", we1[:, 2, :], D)], None, H),
            "l1s": ([("AG", we2, H)], None, D),
            "l1h": ([("NW", wn1[:, 0, :], D), ("XR", wn1[:, 1, :], D)], BN1, H),
            "l1o": ([("NV", wn2, H)], BN2, D),
            "l2k": ([("XR", wks, D)], BKS, H),
            "l2q": ([("XR", wqv, D)], BQV, H),
        }
        ORDER = list(LIN)
        arrays = {"NW": NW, "XR": XR, "NV": NV}
        made = {}
        count = 0
        for name in ORDER:
            made[name] = count
            count += STEPS * len(LIN[name][0])

        def columns(which, i, w):
            if which == "AG":
                return AG[:, bass.ds(i * (GROUP * H), GROUP * H)].rearrange("p (b f) -> p b f", b=GROUP)
            return arrays[which][:, bass.ds(i * GROUP, GROUP), 0:w]

        PRODUCTS = [0, 1, 2, 3, 6]
        SLOT_PASSES = [4, 5]
        FAST = list(range(7))
        GB = NB * NC
        GENERAL = [k for k in range(7) if k not in FAST] or list(range(7))
        OWN_STEPS = [4, 4, 4, 4, 7, 5, 4]
        TILES = {k: ET * sum(j < k for j in GENERAL) for k in range(7)}
        DONE = {k: sum(j < k for j in GENERAL) + 1 for k in range(7)}
        VSTEPS = {k: ET * sum(OWN_STEPS[j] for j in GENERAL if j < k) for k in range(7)}
        BY_DST = [True, False, True, False, True, True, False]
        nodes = lambda ap: ap.rearrange("(p b) f -> p (b f)", p=P)

        def later(w, c, n):
            return not isinstance(w, int) or w * NC + c >= n

        def blocks(eng, body):
            body(0, 0, first=True)
            body(1, 1)
            body(2, 0)
            with eng.Fori(2, NB // 2 + 1) as i:
                body(i * 2 - 1, 1)
                body(i * 2, 0)

        @block.sync
        def _(sp):
            n = 0
            with nc.allow_non_contiguous_dma(reason="small weights"):
                for to, of in ((w1[:, :], W1), (w2[:, :], W2), (we1[:, :, :], We1.rearrange("(c d) h -> d c h", c=3)),
                               (we2[:, :], We2), (wn1[:, :, :], Wn1.rearrange("(c d) h -> d c h", c=2)),
                               (wn2[:, :], Wn2), (wks[:, 0:D], Wk), (wks[:, D:H], Ws),
                               (wqv[:, 0:D], Wq), (wqv[:, D:H], Wv)):
                    sp.dma_start(to, of).then_inc(weights_in, 16)
                    n += 16
                for row, c0, of in ((B1, 0, b1), (B2, 0, b2), (BE1, 0, be1), (BN1, 0, bn1), (BN2, 0, bn2),
                                    (BKS, 0, bk), (BKS, D, bs), (BQV, 0, bq), (BQV, D, bv)):
                    w = of.shape[0]
                    sp.dma_start(brow[0:1, row, c0:c0 + w], of.rearrange("(a n) -> a n", a=1)).then_inc(weights_in, 16)
                    n += 16
                sp.dma_start(be2b[:, :], be2.rearrange("(a n) -> a n", a=1).to_broadcast((P, D))).then_inc(weights_in, 16)
                n += 16
            assert n == WEIGHTS
            sp.dma_start(idst[:, :], dst.rearrange("(p t) -> p t", p=EP)).then_inc(edges_in, 16)
            sp.wait_ge(pool_const, 2)
            sp.dma_start(XR[0:FULL, :, :], x[0:FULL * NB, :].rearrange("(p b) f -> p b f", p=FULL)).then_inc(x_in, 16)
            sp.dma_start(XR[FULL:FULL + 1, 0:REST, :],
                         x[FULL * NB:N, :].rearrange("(p b) f -> p b f", p=1)).then_inc(x_in, 16)
            sp.wait_ge(start_ready, 1)
            with sp.Fori(0, NB) as w:
                first = sp.value_load(start_i[0:1, bass.ds(w, 1)], min_val=0, max_val=E - WE)
                sp.dma_start(srcw[:, bass.ds(w * WT, WT)], src[bass.ds(first, WE)].rearrange("(p t) -> p t", p=P))\
                    .then_inc(window_in, 16)
                sp.dma_start(dstw[:, bass.ds(w * WT, WT)], dst[bass.ds(first, WE)].rearrange("(p t) -> p t", p=P))\
                    .then_inc(window_in, 16)
            for i in range(NC):
                z = feat_slot[i * (FROWS // NC):(i + 1) * (FROWS // NC), :].rearrange("(p r) f -> p r f", p=P)
                sp.dma_start(z, zero[:, 0:D].rearrange("p (a f) -> p a f", a=1).to_broadcast((P, FROWS // NC // P, D)))\
                    .then_inc(filled[int(i > 0)], 16)
            sp.wait_ge(tab_ready, 1)
            sp.dma_start(nodes(tab[0]), TB).then_inc(tab_stored[0], 16)
            sp.wait_ge(rows_kept, NB)
            sp.dma_start(slot_rows.rearrange("w k s -> k w s"), rowsT.rearrange("k (w s) -> k w s", w=NB))\
                .then_inc(rows_stored, 16)
            def store_counts(w):
                for c in range(NC):
                    at = slice(c * CH * P, (c + 1) * CH * P)
                    sp.wait_ge(ct_kept, w * NC + (c + 1))
                    sp.dma_start(cnt_t[bass.ds(w, 1), :, at].rearrange("a p n -> p (a n)"), ct_c[c]).then_inc(cnt_stored[c], 16)
                    sp.wait_ge(cs_kept, w * NC + (c + 1))
                    sp.dma_start(cnt_s[bass.ds(w, 1), :, at].rearrange("a p n -> p (a n)"), cs_c[c]).then_inc(cnt_stored[c], 16)
            with sp.Fori(0, NB) as w:
                store_counts(w)
            for c in range(NC):
                sp.wait_ge(cnt_stored[c], 32 * NB)
            sp.wait_ge(flag_ready, 1)
            fast = sp.value_load(flag_i[0:1, 0:1], min_val=0, max_val=1)

            def product(k):
                w_ = W_TAB[k]
                n = PRODUCTS.index(k)
                table = tab[k].rearrange("(p b) f -> p b f", p=P) if BY_DST[k] else tab[k].rearrange("(b p) f -> p b f", p=P)
                sp.wait_ge(tab_stored[k], 16)
                sp.dma_start(ptab[:, 0:NB * w_].rearrange("p (b f) -> p b f", b=NB), table).then_inc(ptab_in, 16)
                counts = cnt_s if BY_DST[k] else cnt_t

                def load(w):
                    for c in range(NC):
                        if not isinstance(w, int) or w > 0 or n > 0:
                            sp.wait_ge(ring_used, w * NC + (n * NB * NC + c + 1 - NC))
                        sp.dma_start(cring[c], counts[bass.ds(w, 1), :, c * CH * P:(c + 1) * CH * P].rearrange("a p n -> p (a n)"))\
                            .then_inc(ring_in[c], 16)
                load(0)
                with sp.Fori(1, NB) as w:
                    load(w)
                if BY_DST[k]:
                    nth = sum(BY_DST[j] for j in PRODUCTS[:n]) + 1
                    sp.wait_ge(y_all, nth)
                    sp.dma_start(acc[k][0:NP, :].rearrange("(b p) f -> p b f", p=P),
                                 ysum[:, 0:NB * w_].rearrange("p (b f) -> p b f", b=NB)).then_inc(y_stored, 16)
                    sp.wait_ge(y_stored, 16 * nth)
                    sp.dma_start(AG[:, 0:NB * w_], nodes(acc[k][0:NP, :])).then_inc(agg_in[k], 16)

            def slots(k):
                m = SLOT_PASSES.index(k)
                w_ = W_TAB[k]
                sp.wait_ge(tab_stored[k], 32)
                for h in range(2):
                    sp.wait_ge(feat_put[h], 16 * WT * (NB // 2 + 1 - h))
                sp.dma_start(dtab[:, 0:NB * w_].rearrange("p (b f) -> p b f", b=NB), tab[k].rearrange("(b p) f -> p b f", p=P))\
                    .then_inc(tabs_in[0], 16)
                sp.dma_start(qtab, nodes(tab_src[k])).then_inc(tabs_in[1], 16)
                sp.wait_ge(splits_lo, 2 * NC * (m + 1))

                def load(w):
                    for c in range(NC):
                        if not isinstance(w, int):
                            sp.wait_ge(pre_made, w * NC + (m * GB + c + 1 - NC))
                        for kk, to in ((0, selS[c]), (1, selT[c])):
                            row = slot_rows[bass.ds(w, 1), kk * NB + c * CH:kk * NB + (c + 1) * CH, :]
                            sp.dma_start(to, row.rearrange("a k s -> a (k s)").to_broadcast((P, CH * P))).then_inc(slot_in[c], 16)
                        if k == 4:
                            fs = feat_slot.rearrange("(w p b) f -> w p (b f)", w=NB, p=P)
                            sp.dma_start(fslot[c], fs[bass.ds(w, 1), :, c * CH * D:(c + 1) * CH * D].rearrange("a p n -> p (a n)"))\
                                .then_inc(slot_in[c], 16)

                def store(w):
                    sp.wait_ge(zb_kept, w + (m * NB + 1))
                    sp.dma_start(acc[k][bass.ds(w * P, P), :], ystage[:, 0:w_]).then_inc(y_stored, 16)

                load(0)
                with sp.Fori(1, NB) as w:
                    load(w)
                    store(w - 1)
                store(NB - 1)
                sp.wait_ge(y_stored, 16 * (2 + NB * (m + 1)))
                sp.dma_start(AG[:, 0:NB * w_], nodes(acc[k][0:NP, :])).then_inc(agg_in[k], 16)

            def general(k):
                w = W_TAB[k]
                sp.wait_ge(tab_stored[k], 32 if k in (4, 5) else 16)
                z = acc[k].rearrange("(r p) f -> p r f", p=P)
                sp.dma_start(z, zero[:, 0:w].rearrange("p (a w) -> p a w", a=1).to_broadcast((P, NB + 1, w)))\
                    .then_inc(zeroed[k], 16)
                sp.dma_start(isrc, src.rearrange("(p t) -> p t", p=EP)).then_inc(edges2_in[k], 16)
                sp.dma_start(idst, dst.rearrange("(p t) -> p t", p=EP)).then_inc(edges2_in[k], 16)
                if k == 4:
                    ftv = feat.rearrange("(p t) f -> p t f", p=EP)
                    with sp.Fori(0, ET) as t:
                        sp.wait_ge(tile_done, t + (TILES[4] + DONE[4]))
                        sp.dma_start(ft[:, :], ftv[:, bass.ts(t, 1), :].rearrange("p a f -> p (a f)")).then_inc(ft_in, 16)
                sp.wait_ge(added[k], 16 * ET)
                sp.dma_start(AG[:, 0:NB * w], nodes(acc[k][0:NP, :])).then_inc(agg_in[k], 16)

            for k in range(7):
                w = W_TAB[k]
                if k > 0:
                    sp.wait_ge(tab_ready, k + 1)
                if k == 0:
                    pass
                elif k < 2:
                    sp.dma_start(nodes(tab[k]), TB).then_inc(tab_stored[k], 16)
                elif k == 4:
                    sp.dma_start(nodes(tab[4]), NW[:, :, :].rearrange("p b f -> p (b f)")).then_inc(tab_stored[k], 16)
                    sp.dma_start(nodes(tab_src[4]), NV[:, :, :].rearrange("p b f -> p (b f)")).then_inc(tab_stored[k], 16)
                elif k == 5:
                    sp.dma_start(tab[5].rearrange("(p b) f -> p b f", p=P), NW[:, :, 0:D]).then_inc(tab_stored[k], 16)
                    sp.dma_start(nodes(tab_src[5]), NV[:, :, :].rearrange("p b f -> p (b f)")).then_inc(tab_stored[k], 16)
                else:
                    sp.dma_start(tab[k].rearrange("(p b) f -> p b f", p=P), NW[:, :, 0:D]).then_inc(tab_stored[k], 16)
                if k in FAST:
                    with sp.If(fast):
                        (slots if k in SLOT_PASSES else product)(k)
                    with sp.If(1 - fast):
                        general(k)
                else:
                    general(k)
            sp.wait_ge(out_ready, 1)
            sp.dma_start(out[0:FULL * NB, :].rearrange("(p b) f -> p b f", p=FULL), XR[0:FULL, :, :]).then_inc(out_stored, 16)
            sp.dma_start(out[FULL * NB:N, :].rearrange("(p b) f -> p b f", p=1),
                         XR[FULL:FULL + 1, 0:REST, :]).then_inc(out_stored, 16)
            sp.wait_ge(out_stored, 32)

        @block.gpsimd
        def _(pool):
            pool.memset(zero[:, :], 0.0).then_inc(pool_const, 1)
            pool.memset(XR[:, :, :], 0.0).then_inc(pool_const, 1)
            pool.memset(ident[:, :], 0.0).then_inc(pool_const, 1)
            pool.memset(lower[:, :], 0.0).then_inc(pool_const, 1)
            pool.memset(ones_row[:, :], 1.0).then_inc(pool_const, 1)
            pool.memset(epsc[:, 0:1], EPS).then_inc(pool_const, 1)
            pool.memset(epsc[:, 1:2], DEG_EPS).then_inc(pool_const, 1)
            pool.wait_ge(pool_const, 4)
            pool.affine_select(out=ident[:, :], in_=ident[:, :], compare_op=ALU.not_equal, fill=1.0,
                               base=0, pattern=[[-1, P]], channel_multiplier=1).then_inc(pool_const, 1)
            pool.affine_select(out=lower[:, :], in_=lower[:, :], compare_op=ALU.is_ge, fill=1.0,
                               base=0, pattern=[[1, P]], channel_multiplier=-1).then_inc(pool_const, 1)
            pool.iota(rowid[:, :], pattern=[[0, 1]], base=NP, channel_multiplier=1,
                      allow_small_or_imprecise_dtypes=True).then_inc(pool_const, 1)

            def general(k):
                w = W_TAB[k]
                pool.wait_ge(tab_stored[k], 32 if k in (4, 5) else 16)
                idx = lambda c: bass.IndirectOffsetOnAxis(ap=gcol[:, c:c + 1].bitcast(u32), axis=0)
                pool.wait_ge(zeroed[k], 16)
                pool.memset(mark[:, k:k + 1], 0.0).then_inc(tile_done, 1)
                with pool.Fori(0, ET) as t:
                    pool.wait_ge(cols, t + (TILES[k] + 1))
                    pool.nop(nofuse=True)
                    if k in (4, 5):
                        pool.indirect_dma_start(msg[:, 0:w], None, tab[k], idx(0)).then_inc(gathered[k], 16)
                        pool.indirect_dma_start(msg2[:, 0:H], None, tab_src[k], idx(1)).then_inc(gathered[k], 16)
                    else:
                        pool.indirect_dma_start(msg[:, 0:w], None, tab[k], idx(1 if BY_DST[k] else 0))\
                            .then_inc(gathered[k], 16)
                    pool.wait_ge(tot_ready, t + (TILES[k] + 1))
                    pool.nop(nofuse=True)
                    pool.indirect_dma_start(acc[k], bass.IndirectOffsetOnAxis(ap=sidx[:, 0:1].bitcast(u32), axis=0),
                                            tot[:, 0:w], None, compute_op=ALU.add).then_inc(added[k], 16)
                    pool.wait_ge(added[k], 16 * t + 16)
                    pool.nop(nofuse=True)
                    pool.memset(mark[:, k:k + 1], 0.0).then_inc(tile_done, 1)

            def last_parts():
                n = CH * W_TAB[5]

                def body(w, odd, first=False):
                    for c in range(NC):
                        i = (c + odd) % 2
                        pool.wait_ge(msg_mid, w * NC + (GB + c + 1))
                        pool.tensor_tensor(parts3[i][:, 2 * n:3 * n], hid[i][:, 0:n], parts3[i][:, n:2 * n], ALU.subtract)\
                            .then_inc(msg_lo, 1)
                blocks(pool, body)

            pool.memset(identb[:, :], 0.0).then_inc(const_ready, 1)
            pool.memset(upperb[:, :], 0.0).then_inc(const_ready, 1)
            pool.memset(ones_col[:, :], 1.0).then_inc(const_ready, 1)
            pool.memset(sd1[:, :], 0.0).then_inc(const_ready, 1)
            pool.iota(iota1[:, :], pattern=[[1, P]], base=1, channel_multiplier=0,
                      allow_small_or_imprecise_dtypes=True).then_inc(const_ready, 1)
            for to, step_, base in ((wcol, 1, 0), (wfirst, P, 0), (wrow, NP, -NB)):
                pool.iota(to[:, :], pattern=[[step_, NB]], base=base, channel_multiplier=0,
                          allow_small_or_imprecise_dtypes=True).then_inc(const_ready, 1)
            pool.iota(spare[:, :], pattern=[[0, 1]], base=FROWS, channel_multiplier=1,
                      allow_small_or_imprecise_dtypes=True).then_inc(const_ready, 1)
            pool.iota(pnum1[:, :], pattern=[[0, 1]], base=1, channel_multiplier=1,
                      allow_small_or_imprecise_dtypes=True).then_inc(const_ready, 1)
            pool.wait_ge(const_ready, 10)
            pool.affine_select(out=identb[:, :], in_=identb[:, :], compare_op=ALU.not_equal, fill=1.0,
                               base=0, pattern=[[-1, P]], channel_multiplier=1).then_inc(const_ready, 1)
            pool.affine_select(out=upperb[:, :], in_=upperb[:, :], compare_op=ALU.is_ge, fill=1.0,
                               base=0, pattern=[[-1, P]], channel_multiplier=1).then_inc(const_ready, 1)
            pool.wait_ge(start_ready, 1)
            pool.iota(classes.rearrange("p (b t) -> p b t", b=NB), pattern=[[1, NB], [0, WT]], base=0, channel_multiplier=0,
                      allow_small_or_imprecise_dtypes=True).then_inc(const_ready, 1)

            pool.wait_ge(filled[0], 16)

            def put_features(w, h, i):
                first = pool.value_load(start_i[0:1, bass.ds(w, 1)], min_val=0, max_val=E - WE)
                if not isinstance(i, int) or i > 0:
                    pool.wait_ge(feat_put[h], 16 * WT * i)
                pool.dma_start(fwin[h].rearrange("p (t f) -> p t f", t=WT),
                               feat[bass.ds(first, WE), :].rearrange("(p t) f -> p t f", p=P)).then_inc(fwin_in[h], 16)
                pool.wait_ge(srow_made, w + 1)
                pool.wait_ge(fwin_in[h], 16 * i + 16)
                pool.tensor_copy(sidx_p[h][:, :], sidx_w[:, bass.ds(w * WT, WT)]).then_inc(sidx_kept, 1)
                pool.wait_ge(sidx_kept, w + 1)
                pool.nop(nofuse=True)
                for t in range(WT):
                    pool.indirect_dma_start(
                        feat_slot, bass.IndirectOffsetOnAxis(ap=sidx_p[h][:, t:t + 1].bitcast(u32), axis=0),
                        fwin[h][:, t * D:(t + 1) * D], None, bounds_check=FROWS - 1, oob_is_err=False)\
                        .then_inc(feat_put[h], 16)

            put_features(0, 0, 0)
            put_features(1, 1, 0)
            with pool.Fori(1, 3) as i:
                put_features(i * 2, 0, i)
                put_features(i * 2 + 1, 1, i)
            pool.wait_ge(filled[1], 16 * (NC - 1))
            with pool.Fori(3, NB // 2) as i:
                put_features(i * 2, 0, i)
                put_features(i * 2 + 1, 1, i)
            put_features(NB - 1, 0, NB // 2)
            pool.wait_ge(flag_ready, 1)
            fast = pool.value_load(flag_i[0:1, 0:1], min_val=0, max_val=1)

            for k in range(7):
                if k == 5:
                    with pool.If(fast):
                        last_parts()
                with pool.If(1 - fast):
                    general(k)

        @block.tensor
        def _(pe):
            pe.wait_ge(pool_const, 10)
            pe.wait_ge(const_ready, 12)
            pe.wait_ge(weights_in, WEIGHTS)

            def linear(name):
                terms, bias, wo = LIN[name]
                at = ORDER.index(name)

                def transposes(i):
                    for a, (which, wt, wi) in enumerate(terms):
                        pe.wait_ge(xT_copied, i * len(terms) + made[name] + a + 1)
                        pe.wait_ge(xG_in, i * len(terms) + made[name] + a + 1)
                        for j in range(GROUP):
                            last = nc.tensor.matmul(PS[0:wi, a * 1024 + j * P:a * 1024 + (j + 1) * P],
                                                    xG[:, a, j * wi:(j + 1) * wi], ident[:, :], start=True, stop=True)
                        last.then_inc(xT_made, 1)

                def products(i, odd):
                    pe.wait_ge(xT_copied, i * len(terms) + (made[name] + len(terms) + 1))
                    pe.wait_ge(lin_kept, i + (at * STEPS + 1))
                    for j in range(GROUP):
                        o = PS[:, 2048 + j * wo:2048 + (j + 1) * wo]
                        for a, (which, wt, wi) in enumerate(terms):
                            last = nc.tensor.matmul(o, xT[odd][0:wi, a, j * P:(j + 1) * P], wt[:, :],
                                                    start=a == 0, stop=bias is None and a == len(terms) - 1)
                        if bias is not None:
                            last = nc.tensor.matmul(o, ones_row[0:1, :], brow[0:1, bias, 0:wo], start=False, stop=True)
                    last.then_inc(lin_made, 1)

                transposes(0)
                with pe.Fori(0, STEPS // 2) as i:
                    transposes(i * 2 + 1)
                    products(i * 2, 0)
                    transposes(i * 2 + 2)
                    products(i * 2 + 1, 1)
                products(STEPS - 1, 0)

            def edge_pass(k):
                w = W_TAB[k]
                with pe.Fori(0, ET) as t:
                    pe.wait_ge(cols, t + (TILES[k] + 1))
                    nc.tensor.matmul(PS[0:EP, 0:EP], scol[:, 0:1].to_broadcast((EP, EP)), ident[0:EP, 0:EP],
                                     start=True, stop=True).then_inc(sT_made, 1)
                    if k == 4:
                        pe.wait_ge(ft_in, 16 * t + 16)
                        nc.tensor.matmul(PS[0:D, 1024:1024 + EP], ft[:, :], ident[0:EP, 0:EP], start=True, stop=True)\
                            .then_inc(ftT_made, 1)
                        pe.wait_ge(ftT_kept, t + 1)
                        nc.tensor.matmul(PS[0:EP, 1536:1536 + H], ftT[:, :], we1[:, 0, :], start=True, stop=True)\
                            .then_inc(fe_made, 1)
                    pe.wait_ge(eq_made, t + (TILES[k] + 1))
                    nc.tensor.matmul(PS[0:EP, 512:512 + w], eq[:, :], msg[:, 0:w], start=True, stop=True)\
                        .then_inc(tot_made, 1)

            def place_edges():
                pe.wait_ge(counted, 1)
                nc.tensor.matmul(PS[0:1, 0:NB], ones_col[0:EP, :], cnt[0:EP, :], start=True, stop=True).then_inc(start_made, 1)
                ohx3 = ohx.rearrange("p (b t) -> p b t", b=NB)
                with pe.Fori(0, NB) as w:
                    pe.wait_ge(oh_made, w + 1)
                    for t in range(WT):
                        last = nc.tensor.matmul(PS[:, 512:512 + NB], upperb[:, :],
                                                ohx3[:, :, 1 + t:2 + t].rearrange("p b a -> p (b a)"),
                                                start=t == 0, stop=t == WT - 1)
                    last.then_inc(before_made, 1)
                    pe.wait_ge(ohr_made, w + 1)
                    for t in range(WT):
                        last = nc.tensor.matmul(PS[:, 1024:1024 + 2 * NB], ohr[:, t * P:(t + 1) * P],
                                                wpay[:, t * 2 * NB:(t + 1) * 2 * NB], start=t == 0, stop=t == WT - 1)
                    last.then_inc(slots_made, 1)
                    pe.wait_ge(sd_kept, w + 1)
                    nc.tensor.matmul(PS[:, 1536:1536 + P], sd1[:, :], identb[:, :], start=True, stop=True).then_inc(rows_made, 1)
                pe.wait_ge(placed_ready, 1)
                nc.tensor.matmul(PS[0:1, 0:1], ones_col[:, :], placed1[:, :], start=True, stop=True).then_inc(total_made, 1)

            def make_counts():
                def body(w):
                    for c in range(NC):
                        pe.wait_ge(hot_made, w * NC + (c + 1))
                        at = (c % 2) * 2048
                        if c >= 2:
                            pe.wait_ge(ct_kept, w * NC + (c - 1))
                            pe.wait_ge(cs_kept, w * NC + (c - 1))
                        elif not isinstance(w, int):
                            pe.wait_ge(ct_kept, w * NC)
                            pe.wait_ge(cs_kept, w * NC)
                        for j in range(CH):
                            cut = slice(j * P, (j + 1) * P)
                            nc.tensor.matmul(PS[:, at + j * P:at + (j + 1) * P], oht_c[c][:, cut], ohs_c[c][:, cut],
                                             start=True, stop=True)
                            last = nc.tensor.matmul(PS[:, at + 1024 + j * P:at + 1024 + (j + 1) * P], ohs_c[c][:, cut],
                                                    oht_c[c][:, cut], start=True, stop=True)
                        last.then_inc(cnt_made, 1)
                body(0)
                with pe.Fori(1, NB) as w:
                    body(w)

            def product(k):
                w_ = W_TAB[k]
                n = PRODUCTS.index(k)
                pe.wait_ge(split_made, NC * (n + 1))
                split = psplit[:, 0:NB * 3 * w_]

                def by_target(w):
                    m = sum(BY_DST[j] for j in PRODUCTS[:n])
                    for c in range(NC):
                        half = int(c >= 4)
                        if c in (0, 4) and (not isinstance(w, int) or m > 0):
                            pe.wait_ge(yb_kept if half else ya_kept, w + m * NB)
                        pe.wait_ge(ring_in[c], 16 * w + 16 * (n * NB + 1))
                        for j in range(CH):
                            for s in range(3):
                                b = c * CH + j
                                last = nc.tensor.matmul(PS[:, half * 512:half * 512 + w_], cring[c][:, j * P:(j + 1) * P],
                                                        split[:, (b * 3 + s) * w_:(b * 3 + s + 1) * w_],
                                                        start=c in (0, 4) and j == 0 and s == 0,
                                                        stop=c in (3, 6) and j == CH - 1 and s == 2)
                        last.then_inc(ring_used, 1)

                def by_source(w, first):
                    for c in range(NC):
                        pe.wait_ge(ring_in[c], 16 * w + 16 * (n * NB + 1))
                        for j in range(CH):
                            for s in range(3):
                                last = nc.tensor.matmul(PS[:, c * 512 + j * w_:c * 512 + (j + 1) * w_], cring[c][:, j * P:(j + 1) * P],
                                                        split[:, bass.ds(w * (3 * w_) + s * w_, w_)],
                                                        start=first and j == 0 and s == 0, stop=False, skip_group_check=True)
                        last.then_inc(ring_used, 1)

                if BY_DST[k]:
                    by_target(0)
                    with pe.Fori(1, NB) as w:
                        by_target(w)
                else:
                    by_source(0, True)
                    with pe.Fori(1, NB) as w:
                        by_source(w, False)

            def slots(k):
                m = SLOT_PASSES.index(k)
                w_ = W_TAB[k]
                pe.wait_ge(splits_lo, 2 * NC * (m + 1))

                def transpose_features(w, c):
                    if k != 4:
                        return
                    pe.wait_ge(slot_in[c], 48 * w + 48)
                    if later(w, c, 1):
                        pe.wait_ge(fT_kept, w * NC + c)
                    for j in range(CH):
                        last = nc.tensor.matmul(PS[0:D, 2048 + j * P:2048 + (j + 1) * P], fslot[c][:, j * D:(j + 1) * D], ident[:, :],
                                                start=True, stop=True)
                    last.then_inc(fT_made, 1)

                def meet(w, c, odd):
                    i = (c + odd) % 2
                    at = i * 1024
                    pe.wait_ge(sel_made, w * NC + (m * GB + c + 1))
                    if later(w, c, 2):
                        pe.wait_ge(pre_free, w * NC + (m * GB + c - 1))
                    if k == 4:
                        pe.wait_ge(fT_kept, w * NC + (c + 1))
                    for j in range(CH):
                        cut = slice(j * P, (j + 1) * P)
                        b = c * CH + j
                        for s in range(3):
                            last = nc.tensor.matmul(PS[:, at + j * P:at + (j + 1) * P], selS[c][:, cut],
                                                    qsplit[:, (b * 3 + s) * H:(b * 3 + s + 1) * H],
                                                    start=s == 0, stop=False, skip_group_check=True)
                        for s in range(3):
                            last = nc.tensor.matmul(PS[:, at + j * P:at + j * P + w_], selT[c][:, cut],
                                                    dsplit[:, bass.ds(w * (3 * w_) + s * w_, w_)],
                                                    start=False, stop=k != 4 and s == 2, skip_group_check=True)
                        if k == 4:
                            last = nc.tensor.matmul(PS[:, at + j * P:at + (j + 1) * P], fT[i][:, cut], we1[:, 0, :],
                                                    start=False, stop=True, skip_group_check=True)
                    last.then_inc(pre_made, 1)

                def add_up(w, c, odd):
                    half = int(c >= 4)
                    if c in (0, 4) and (m > 0 or later(w, 0, 1)):
                        pe.wait_ge(zb_kept if half else za_kept, w + m * NB)
                    pe.wait_ge(msg_lo, w * NC + (m * GB + c + 1))
                    for j in range(CH):
                        for s in range(3):
                            last = nc.tensor.matmul(PS[:, 3072 + half * 512:3072 + half * 512 + w_], sumT[c][:, j * P:(j + 1) * P],
                                                    parts3[(c + odd) % 2][:, (s * CH + j) * w_:(s * CH + j + 1) * w_],
                                                    start=c in (0, 4) and j == 0 and s == 0,
                                                    stop=c in (3, 6) and j == CH - 1 and s == 2)
                    last.then_inc(agg_made, 1)

                def body(w, odd, first=False):
                    for c in range(NC):
                        transpose_features(w, c)
                        for lag, part in ((2, meet), (4, add_up)):
                            if c >= lag:
                                part(w, c - lag, odd)
                            elif not first:
                                part(w - 1, NC + c - lag, 1 - odd)
                blocks(pe, body)
                for c in range(NC - 2, NC):
                    meet(NB - 1, c, 0)
                    add_up(NB - 1, c - 2, 0)
                for c in range(NC - 2, NC):
                    add_up(NB - 1, c, 0)

            def fast_or_general(k):
                with pe.If(fast):
                    (slots if k in SLOT_PASSES else product)(k)
                with pe.If(1 - fast):
                    edge_pass(k)

            place_edges()
            make_counts()
            pe.wait_ge(flag_ready, 1)
            fast = pe.value_load(flag_i[0:1, 0:1], min_val=0, max_val=1)
            fast_or_general(0)
            fast_or_general(1)
            linear("l0a")
            fast_or_general(2)
            fast_or_general(3)
            linear("l0b")
            linear("l1p")
            linear("l1q")
            fast_or_general(4)
            linear("l1s")
            linear("l1h")
            linear("l1o")
            linear("l2k")
            linear("l2q")
            fast_or_general(5)
            fast_or_general(6)

        @block.scalar
        def _(act):
            act.wait_ge(pool_const, 7)
            nc.scalar.activation(epsc[0:1, 0:1], epsc[0:1, 0:1], ACT.Copy).then_inc(xT_copied, 1)

            def linear(name):
                terms, bias, wo = LIN[name]

                def copies(i, odd):
                    for a, (which, wt, wi) in enumerate(terms):
                        act.wait_ge(xT_made, i * len(terms) + (made[name] + a + 2))
                        nc.scalar.activation(xT[odd][0:wi, a, :], PS[0:wi, a * 1024:a * 1024 + GROUP * P], ACT.Copy)\
                            .then_inc(xT_copied, 1)

                with act.Fori(0, STEPS // 2) as i:
                    copies(i * 2, 0)
                    copies(i * 2 + 1, 1)
                copies(STEPS - 1, 0)

            def norm(n):
                act.wait_ge(std_in, n + 1)
                nc.scalar.activation(st[:, TMP, :], st[:, VAR, :], ACT.Sqrt, bias=epsc[:, 0:1], scale=1.0 / D)\
                    .then_inc(std_out, 1)

            def gates():
                with act.Fori(0, ET) as t:
                    act.wait_ge(gate_in, t + 1)
                    nc.scalar.activation(msg[:, 0:D], msg[:, 0:D], ACT.Sigmoid).then_inc(gate_out, 1)

            def place_edges():
                ohx3 = ohx.rearrange("p (b t) -> p b t", b=NB)
                with act.Fori(0, NB) as w:
                    act.wait_ge(before_made, w + 1)
                    nc.scalar.activation(ohx3[:, :, 0:1], PS[:, 512:512 + NB].rearrange("p (b a) -> p b a", a=1), ACT.Copy)\
                        .then_inc(before_kept, 1)
                    act.wait_ge(slots_made, w + 1)
                    nc.scalar.activation(sd1[:, 0:2 * NB], PS[:, 1024:1024 + 2 * NB], ACT.Copy)
                    nc.scalar.activation(SD[:, bass.ds(w * (2 * NB), 2 * NB)], PS[:, 1024:1024 + 2 * NB], ACT.Copy)\
                        .then_inc(sd_kept, 1)
                    act.wait_ge(rows_made, w + 1)
                    nc.scalar.activation(rowsT[:, bass.ds(w * P, P)], PS[0:2 * NB, 1536:1536 + P], ACT.Copy)\
                        .then_inc(rows_kept, 1)

            def make_counts():
                def body(w):
                    for c in range(NC):
                        if not isinstance(w, int):
                            act.wait_ge(cnt_stored[c], 32 * w)
                        act.wait_ge(cnt_made, w * NC + (c + 1))
                        at = (c % 2) * 2048
                        nc.scalar.activation(ct_c[c], PS[:, at:at + CH * P], ACT.Copy).then_inc(ct_kept, 1)
                        nc.scalar.activation(cs_c[c], PS[:, at + 1024:at + 1024 + CH * P], ACT.Copy).then_inc(cs_kept, 1)
                body(0)
                with act.Fori(1, NB) as w:
                    body(w)

            def product(k):
                w_ = W_TAB[k]
                n = PRODUCTS.index(k)
                act.wait_ge(ptab_in, 16 * (n + 1))
                tabs = ptab[:, 0:NB * w_].rearrange("p (b f) -> p b f", b=NB)
                ress = pres[:, 0:NB * w_].rearrange("p (b f) -> p b f", b=NB)
                parts = psplit[:, 0:NB * 3 * w_].rearrange("p (b s f) -> p b s f", b=NB, s=3)
                with act.Fori(0, NC) as c:
                    at = bass.ds(c * CH, CH)
                    nc.scalar.activation(parts[:, at, 0, :], tabs[:, at, :], ACT.Copy).then_inc(hi_made, 1)
                with act.Fori(0, NC) as c:
                    at = bass.ds(c * CH, CH)
                    act.wait_ge(res_made, c + (n * NC + 1))
                    nc.scalar.activation(parts[:, at, 1, :], ress[:, at, :], ACT.Copy).then_inc(mid_made, 1)
                if BY_DST[k]:
                    m = sum(BY_DST[j] for j in PRODUCTS[:n])
                    def keep_first_part(w):
                        if not isinstance(w, int) or m > 0:
                            act.wait_ge(yb_kept, w + m * NB)
                        act.wait_ge(ring_used, w * NC + (n * NB * NC + 4))
                        nc.scalar.activation(y0[:, 0:w_], PS[:, 0:w_], ACT.Copy).then_inc(ya_kept, 1)
                    keep_first_part(0)
                    with act.Fori(1, NB) as w:
                        keep_first_part(w)

            def slots(k):
                m = SLOT_PASSES.index(k)
                w_ = W_TAB[k]
                for i, (tb, sp_, wd) in enumerate(((dtab, dsplit, w_), (qtab, qsplit, H))):
                    act.wait_ge(tabs_in[i], 16 * (m + 1))
                    t3 = tb[:, 0:NB * wd].rearrange("p (b f) -> p b f", b=NB)
                    s3 = sp_[:, 0:NB * 3 * wd].rearrange("p (b s f) -> p b s f", b=NB, s=3)
                    with act.Fori(0, NC) as c:
                        nc.scalar.activation(s3[:, bass.ds(c * CH, CH), 0, :], t3[:, bass.ds(c * CH, CH), :], ACT.Copy)\
                            .then_inc(splits_hi, 1)
                    with act.Fori(0, NC) as c:
                        act.wait_ge(splits_res, c + (1 + NC * (2 * m + i)))
                        nc.scalar.activation(s3[:, bass.ds(c * CH, CH), 1, :], t3[:, bass.ds(c * CH, CH), :], ACT.Copy)\
                            .then_inc(splits_mid, 1)

                def keep_features(w, c, odd):
                    if k != 4:
                        return
                    act.wait_ge(fT_made, w * NC + (c + 1))
                    if later(w, c, 2):
                        act.wait_ge(pre_made, w * NC + (c - 1))
                    nc.scalar.activation(fT[(c + odd) % 2], PS[0:D, 2048:2048 + CH * P], ACT.Copy).then_inc(fT_kept, 1)

                def messages(w, c, odd):
                    i = (c + odd) % 2
                    at = i * 1024
                    n = CH * w_
                    act.wait_ge(pre_made, w * NC + (m * GB + c + 1))
                    if later(w, c, 2):
                        act.wait_ge(agg_made, w * NC + (m * GB + c - 1))
                    if k == 4:
                        nc.scalar.activation(hid[i], PS[:, at:at + CH * P], ACT.Relu).then_inc(msg_made, 1)
                        nc.scalar.activation(parts3[i][:, 0:n], PS[:, at:at + CH * P], ACT.Relu).then_inc(pre_free, 1)
                    else:
                        pre3 = PS[:, at:at + CH * P].rearrange("p (j f) -> p j f", j=CH)
                        nc.scalar.activation(hid[i][:, 0:n].rearrange("p (j f) -> p j f", j=CH), pre3[:, :, 0:D], ACT.Sigmoid)\
                            .then_inc(gate_made, 1)
                        act.wait_ge(pre_free, w * NC + (GB + c + 1))
                        nc.scalar.activation(parts3[i][:, 0:n], hid[i][:, 0:n], ACT.Copy).then_inc(msg_hi, 1)
                    act.wait_ge(msg_res, w * NC + (m * GB + c + 1))
                    nc.scalar.activation(parts3[i][:, n:2 * n], hid[i][:, 0:n], ACT.Copy).then_inc(msg_mid, 1)

                def first_part(w):
                    if m > 0 or later(w, 0, 1):
                        act.wait_ge(zb_kept, w + m * NB)
                    act.wait_ge(agg_made, w * NC + (m * GB + 4))
                    nc.scalar.activation(y0[:, 0:w_], PS[:, 3072:3072 + w_], ACT.Copy).then_inc(za_kept, 1)

                def body(w, odd, first=False):
                    for c in range(NC):
                        keep_features(w, c, odd)
                        if c >= 2:
                            messages(w, c - 2, odd)
                        elif not first:
                            messages(w - 1, NC + c - 2, 1 - odd)
                    first_part(w)
                blocks(act, body)
                messages(NB - 1, NC - 2, 0)
                messages(NB - 1, NC - 1, 0)

            def fast_or_general(k):
                with act.If(fast):
                    (slots if k in SLOT_PASSES else product)(k)
                if k == 5:
                    with act.If(1 - fast):
                        gates()

            place_edges()
            make_counts()
            act.wait_ge(flag_ready, 1)
            fast = act.value_load(flag_i[0:1, 0:1], min_val=0, max_val=1)
            fast_or_general(0)
            fast_or_general(1)
            linear("l0a")
            fast_or_general(2)
            fast_or_general(3)
            linear("l0b")
            norm(0)
            linear("l1p")
            linear("l1q")
            fast_or_general(4)
            linear("l1s")
            linear("l1h")
            linear("l1o")
            norm(1)
            linear("l2k")
            linear("l2q")
            fast_or_general(5)
            norm(2)
            act.wait_ge(std_in, 4)
            nc.scalar.activation(st[:, TMP, :], st[:, SUM, :], ACT.Sqrt, bias=epsc[:, 1:2]).then_inc(std_out, 1)
            fast_or_general(6)
            norm(4)

        @block.vector
        def _(dve):
            done = [0]

            def step(ins):
                done[0] += 1
                ins.then_inc(dve_step, 1)
                dve.wait_ge(dve_step, done[0])

            V = nc.vector
            step(V.memset(st[:, :, :], 0.0))
            V.memset(gcol[:, :], 0).then_inc(xT_made, 1)
            V.memset(TB, 1.0).then_inc(lin_kept, 1)

            def per_node(row, w):
                return st[:, row, :].rearrange("p (b a) -> p b a", a=1).to_broadcast((P, NB, w))

            def keep(name, to, relu=False):
                terms, bias, wo = LIN[name]
                at = ORDER.index(name)

                def bring(i):
                    for a, (which, wt, wi) in enumerate(terms):
                        dve.wait_ge(xT_made, i * len(terms) + (made[name] + 1))
                        V.tensor_copy(xG[:, a, 0:GROUP * wi].rearrange("p (b f) -> p b f", b=GROUP),
                                      columns(which, i, wi)).then_inc(xG_in, 1)

                def take(i):
                    dve.wait_ge(lin_made, i + (at * STEPS + 1))
                    o = PS[:, 2048:2048 + GROUP * wo].rearrange("p (b f) -> p b f", b=GROUP)
                    t = to[:, bass.ds(i * GROUP, GROUP), 0:wo]
                    V.tensor_scalar(t, o, 0.0 if relu else 1.0, None, ALU.max if relu else ALU.mult).then_inc(lin_kept, 1)

                dve.wait_ge(lin_in, at + 1)
                bring(0)
                with dve.Fori(0, STEPS - 1) as i:
                    bring(i + 1)
                    take(i)
                take(STEPS - 1)
                dve.wait_ge(lin_kept, (at + 1) * STEPS + 1)

            norms = [0]

            def root():
                norms[0] += 1
                dve.wait_ge(std_out, norms[0])

            def layer_norm():
                step(V.tensor_reduce(st[:, SUM, :], XR[:, :, :], AX.X, ALU.add))
                step(V.tensor_scalar(st[:, SUM, :], st[:, SUM, :], 1.0 / D, None, ALU.mult))
                step(V.tensor_tensor(XR[:, :, :], XR[:, :, :], per_node(SUM, D), ALU.subtract))
                step(V.tensor_tensor(NV[:, :, 0:D], XR[:, :, :], XR[:, :, :], ALU.mult))
                V.tensor_reduce(st[:, VAR, :], NV[:, :, 0:D], AX.X, ALU.add).then_inc(std_in, 1)
                root()
                step(V.reciprocal(st[:, TMP, :], st[:, TMP, :]))
                step(V.tensor_tensor(XR[:, :, :], XR[:, :, :], per_node(TMP, D), ALU.mult))

            def inverse(to, of):
                step(V.tensor_scalar(st[:, TMP, :], st[:, of, :], 1.0, None, ALU.max))
                step(V.reciprocal(st[:, TMP, :], st[:, TMP, :]))
                step(V.tensor_scalar(st[:, to, :], st[:, of, :], 0.0, None, ALU.is_gt))
                step(V.tensor_tensor(st[:, to, :], st[:, to, :], st[:, TMP, :], ALU.mult))

            def edge_pass(k):
                w = W_TAB[k]
                steps = OWN_STEPS[k]
                by = idst if BY_DST[k] else isrc
                dve.wait_ge(edges2_in[k], 32)
                with dve.Fori(0, ET) as t:
                    n = [0]

                    def own(ins):
                        n[0] += 1
                        ins.then_inc(vec, 1)
                        dve.wait_ge(vec, t * steps + (VSTEPS[k] + n[0]))

                    dve.wait_ge(tile_done, t + (TILES[k] + DONE[k]))
                    V.tensor_copy(gcol[:, 0:1], idst[:, bass.ts(t, 1)])
                    V.tensor_copy(gcol[:, 1:2], isrc[:, bass.ts(t, 1)])
                    own(V.tensor_copy(scol[:, :], by[:, bass.ts(t, 1)]))
                    V.tensor_scalar(slot[:, :], scol[:, :], -1.0, rowid[:, :], ALU.mult, ALU.add).then_inc(cols, 1)
                    dve.wait_ge(sT_made, t + (TILES[k] + 1))
                    own(V.tensor_scalar(eq[:, :], PS[0:EP, 0:EP], scol[:, 0:1], None, ALU.is_equal))
                    own(V.tensor_tensor(eqlow[:, :], eq[:, :], lower[0:EP, 0:EP], ALU.mult))
                    own(V.tensor_reduce(dup[:, 0:1], eqlow[:, :], AX.X, ALU.max))
                    if k == 4:
                        dve.wait_ge(ftT_made, t + 1)
                        V.tensor_copy(ftT[:, :], PS[0:D, 1024:1024 + EP]).then_inc(ftT_kept, 1)
                        dve.wait_ge(gathered[k], 32 * t + 32)
                        own(V.tensor_tensor(msg[:, 0:H], msg[:, 0:H], msg2[:, :], ALU.add))
                        dve.wait_ge(fe_made, t + 1)
                        own(V.tensor_tensor(msg[:, 0:H], msg[:, 0:H], PS[0:EP, 1536:1536 + H], ALU.add))
                        own(V.tensor_scalar(msg[:, 0:H], msg[:, 0:H], 0.0, None, ALU.max))
                    elif k == 5:
                        dve.wait_ge(gathered[k], 32 * t + 32)
                        V.tensor_tensor(msg[:, 0:D], msg[:, 0:D], msg2[:, 0:D], ALU.add).then_inc(gate_in, 1)
                        dve.wait_ge(gate_out, t + 1)
                        own(V.tensor_tensor(msg[:, 0:D], msg[:, 0:D], msg2[:, D:H], ALU.mult))
                    else:
                        dve.wait_ge(gathered[k], 16 * t + 16)
                    V.scalar_tensor_tensor(sidx[:, :], dup[:, 0:1], slot[:, 0:1], scol[:, :], ALU.mult, ALU.add)\
                        .then_inc(eq_made, 1)
                    dve.wait_ge(tot_made, t + (TILES[k] + 1))
                    V.tensor_copy(tot[:, 0:w], PS[0:EP, 512:512 + w]).then_inc(tot_ready, 1)

            def count_blocks():
                dve.wait_ge(edges_in, 16)
                dve.wait_ge(const_ready, 12)
                step(V.tensor_scalar(isrc, idst, 7, None, ALU.logical_shift_right))
                step(V.tensor_copy(blk, isrc))
                with dve.Fori(0, NB) as w:
                    V.tensor_scalar(prod_junk, blk, wcol[0:EP, bass.ds(w, 1)], 0.0, ALU.is_lt, ALU.add,
                                    accum_out=cnt[0:EP, bass.ds(w, 1)]).then_inc(slot_step, 1)
                    dve.wait_ge(slot_step, w + 1)
                V.memset(vmark[:, :], 0.0).then_inc(counted, 1)
                dve.wait_ge(start_made, 1)
                V.tensor_scalar(start_i[:, :], PS[0:1, 0:NB], float(E - WE), None, ALU.min).then_inc(start_ready, 1)

            def place_edges():
                dve.wait_ge(const_ready, 13)
                dve.wait_ge(window_in, 32 * NB)
                TS, STT, TT = V.tensor_scalar, V.scalar_tensor_tensor, V.tensor_tensor
                step(V.tensor_copy(t_f, srcw))
                step(TS(q_i, t_f, 1.0 / NB, None, ALU.mult))
                step(V.tensor_copy(q_f, q_i))
                step(STT(r_f, q_f, -float(NB), t_f, ALU.mult, ALU.add))
                step(TS(t_f, r_f, 0.0, None, ALU.is_lt))
                step(TT(q_f, q_f, t_f, ALU.subtract))
                step(STT(r_f, t_f, float(NB), r_f, ALU.mult, ALU.add))
                step(TS(t_f, r_f, float(NB), None, ALU.is_ge))
                step(TT(q_f, q_f, t_f, ALU.add))
                step(STT(r_f, t_f, -float(NB), r_f, ALU.mult, ALU.add))
                step(TS(pay[:, 0, :], q_f, 1.0, None, ALU.add))
                by_w = lambda a: a.rearrange("p (w t) -> p w t", w=NB)
                over = lambda a: a[:, :].rearrange("p (w a) -> p w a", a=1).to_broadcast((P, NB, WT))
                step(V.tensor_copy(t_f, dstw))
                step(TT(by_w(t_f), by_w(t_f), over(wfirst), ALU.subtract))
                step(TS(q_f, t_f, 0.0, None, ALU.is_ge))
                step(STT(q_f, t_f, float(P - 1), q_f, ALU.is_le, ALU.mult))
                step(TS(pay[:, 1, :], t_f, 1.0, None, ALU.add))
                step(STT(t_f, r_f, 1.0, q_f, ALU.add, ALU.mult))
                step(TS(class_b, t_f, -1.0, None, ALU.add))
                step(TT(by_w(r_f), by_w(r_f), over(wrow), ALU.add))
                step(V.memset(mask, 1.0))
                step(V.memset(mask.rearrange("p (b t) -> p b t", b=NB)[:, :, 0:1], 0.0))
                ohx3 = ohx.rearrange("p (b t) -> p b t", b=NB)[:, :, 1:WT + 1]
                ranks3 = ranks.rearrange("p (b t) -> p b t", b=NB)[:, :, 1:WT + 1]
                steps = 9

                def body(w):
                    n = [0]

                    def own(ins):
                        n[0] += 1
                        ins.then_inc(slot_step, 1)
                        dve.wait_ge(slot_step, w * steps + (NB + n[0]))

                    at = bass.ds(w * WT, WT)
                    own(TT(ohx3, class_b[:, at].rearrange("p (a t) -> p a t", a=1).to_broadcast((P, NB, WT)),
                           classes.rearrange("p (b t) -> p b t", b=NB), ALU.is_equal))
                    V.memset(vmark[:, :], 0.0).then_inc(oh_made, 1)
                    if not isinstance(w, int):
                        dve.wait_ge(slots_made, w)
                    for k in range(2):
                        TT(wpay.rearrange("p (t k b) -> p t k b", t=WT, k=2)[:, :, k, :], ohx3.rearrange("p b t -> p t b"),
                           pay[:, k, at].rearrange("p (t a) -> p t a", a=1).to_broadcast((P, WT, NB)), ALU.mult)
                    dve.wait_ge(before_kept, w + 1)
                    own(V.tensor_tensor_scan(ranks, mask, ohx, 0.0, ALU.mult, ALU.add))
                    own(TT(prod.rearrange("p (t b) -> p t b", t=WT), ranks3.rearrange("p b t -> p t b"),
                           ohx3.rearrange("p b t -> p t b"), ALU.mult))
                    own(V.tensor_reduce(rank[:, :], prod.rearrange("p (t b) -> p t b", t=WT), AX.X, ALU.add))
                    for t in range(WT):
                        last = TS(ohr[:, t * P:(t + 1) * P], iota1[:, :], rank[:, t:t + 1], None, ALU.is_equal)
                    last.then_inc(ohr_made, 1)
                    own(TS(fit[:, 0, :], rank[:, :], 1.0, None, ALU.is_ge))
                    own(STT(fit[:, 1, :], rank[:, :], float(SLOTS), fit[:, 0, :], ALU.is_le, ALU.mult,
                            accum_out=placed[:, bass.ds(w, 1)]))
                    own(STT(srow[:, 0, :], rank[:, :], float(NB), r_f[:, at], ALU.mult, ALU.add))
                    own(STT(srow[:, 1, :], srow[:, 0, :], spare[:, 0:1], fit[:, 1, :], ALU.subtract, ALU.mult))
                    own(TS(sidx_w[:, at], srow[:, 1, :], spare[:, 0:1], None, ALU.add))
                    V.memset(vmark[:, :], 0.0).then_inc(srow_made, 1)

                body(0)
                with dve.Fori(1, NB) as w:
                    body(w)
                V.tensor_reduce(placed1[:, :], placed[:, :], AX.X, ALU.add).then_inc(placed_ready, 1)
                dve.wait_ge(total_made, 1)
                V.tensor_scalar(flag_i[:, :], PS[0:1, 0:1], float(E), None, ALU.is_equal).then_inc(flag_ready, 1)

            def make_counts():
                def body(w):
                    for c in range(NC):
                        if not isinstance(w, int):
                            dve.wait_ge(cnt_made, w * NC + (c + 1 - NC))
                        for k, to in ((0, ohs_c[c]), (1, oht_c[c])):
                            last = V.tensor_tensor(
                                to.rearrange("p (b s) -> p b s", b=CH),
                                SD[:, bass.ds(w * (2 * NB) + k * NB + c * CH, CH)].rearrange("p (b a) -> p b a", a=1)
                                .to_broadcast((P, CH, P)),
                                iota1[:, :].rearrange("p (a s) -> p a s", a=1).to_broadcast((P, CH, P)), ALU.is_equal)
                        last.then_inc(hot_made, 1)

                dve.wait_ge(rows_stored, 16)
                dve.wait_ge(sd_kept, NB)
                body(0)
                with dve.Fori(1, NB) as w:
                    body(w)

            def product(k):
                w_ = W_TAB[k]
                n = PRODUCTS.index(k)
                dve.wait_ge(ptab_in, 16 * (n + 1))
                tabs = ptab[:, 0:NB * w_].rearrange("p (b f) -> p b f", b=NB)
                ress = pres[:, 0:NB * w_].rearrange("p (b f) -> p b f", b=NB)
                parts = psplit[:, 0:NB * 3 * w_].rearrange("p (b s f) -> p b s f", b=NB, s=3)
                with dve.Fori(0, NC) as c:
                    at = bass.ds(c * CH, CH)
                    dve.wait_ge(hi_made, c + (n * NC + 1))
                    V.tensor_tensor(ress[:, at, :], tabs[:, at, :], parts[:, at, 0, :], ALU.subtract).then_inc(res_made, 1)
                with dve.Fori(0, NC) as c:
                    at = bass.ds(c * CH, CH)
                    dve.wait_ge(mid_made, c + (n * NC + 1))
                    V.tensor_tensor(parts[:, at, 2, :], ress[:, at, :], parts[:, at, 1, :], ALU.subtract).then_inc(split_made, 1)
                if BY_DST[k]:
                    m = sum(BY_DST[j] for j in PRODUCTS[:n])
                    with dve.Fori(0, NB) as w:
                        dve.wait_ge(ya_kept, w + (m * NB + 1))
                        dve.wait_ge(ring_used, w * NC + (n * NB * NC + NC))
                        V.tensor_tensor(ysum[:, bass.ds(w * w_, w_)], y0[:, 0:w_], PS[:, 512:512 + w_], ALU.add).then_inc(yb_kept, 1)
                    dve.wait_ge(yb_kept, (m + 1) * NB)
                    V.memset(vmark[:, :], 0.0).then_inc(y_all, 1)
                    dve.wait_ge(agg_in[k], 16)
                else:
                    dve.wait_ge(ring_used, (n + 1) * NB * NC)
                    for c in range(NC):
                        last = V.tensor_copy(AG[:, c * CH * w_:(c + 1) * CH * w_], PS[:, c * 512:c * 512 + CH * w_])
                    last.then_inc(agg_kept, 1)
                    dve.wait_ge(agg_kept, sum(not BY_DST[j] for j in PRODUCTS[:n]) + 1)

            def slots(k):
                m = SLOT_PASSES.index(k)
                w_ = W_TAB[k]
                for i, (tb, sp_, wd) in enumerate(((dtab, dsplit, w_), (qtab, qsplit, H))):
                    t3 = tb[:, 0:NB * wd].rearrange("p (b f) -> p b f", b=NB)
                    s3 = sp_[:, 0:NB * 3 * wd].rearrange("p (b s f) -> p b s f", b=NB, s=3)
                    with dve.Fori(0, NC) as c:
                        at = bass.ds(c * CH, CH)
                        dve.wait_ge(splits_hi, c + (1 + NC * (2 * m + i)))
                        V.tensor_tensor(t3[:, at, :], t3[:, at, :], s3[:, at, 0, :], ALU.subtract).then_inc(splits_res, 1)
                    with dve.Fori(0, NC) as c:
                        at = bass.ds(c * CH, CH)
                        dve.wait_ge(splits_mid, c + (1 + NC * (2 * m + i)))
                        V.tensor_tensor(s3[:, at, 2, :], t3[:, at, :], s3[:, at, 1, :], ALU.subtract).then_inc(splits_lo, 1)

                def select_rows(w, c):
                    dve.wait_ge(slot_in[c], 48 * w + 48 if k == 4 else 32 * w + (48 * NB + 32))
                    V.tensor_scalar(selS[c], selS[c], pnum1[:, 0:1], None, ALU.is_equal)
                    V.tensor_scalar(selT[c], selT[c], pnum1[:, 0:1], None, ALU.is_equal)

                def select_sums(w, c):
                    if later(w, 0, 1):
                        dve.wait_ge(agg_made, w * NC + (m * GB + c + 1 - NC))
                    V.tensor_tensor(sumT[c].rearrange("p (b s) -> p b s", b=CH),
                                    SD[:, bass.ds(w * (2 * NB) + (NB + c * CH), CH)].rearrange("p (b a) -> p b a", a=1)
                                    .to_broadcast((P, CH, P)),
                                    iota1[:, :].rearrange("p (a s) -> p a s", a=1).to_broadcast((P, CH, P)), ALU.is_equal)\
                        .then_inc(sel_made, 1)

                def gate(w, c, odd):
                    if k == 4:
                        return
                    i = (c + odd) % 2
                    pre3 = PS[:, i * 1024:i * 1024 + CH * P].rearrange("p (j f) -> p j f", j=CH)
                    h3 = hid[i][:, 0:CH * D].rearrange("p (j f) -> p j f", j=CH)
                    dve.wait_ge(gate_made, w * NC + (c + 1))
                    V.tensor_tensor(h3, h3, pre3[:, :, D:H], ALU.mult).then_inc(pre_free, 1)

                def residual(w, c, odd):
                    i = (c + odd) % 2
                    dve.wait_ge(*((pre_free, w * NC + (c + 1)) if k == 4 else (msg_hi, w * NC + (c + 1))))
                    V.tensor_tensor(hid[i][:, 0:CH * w_], hid[i][:, 0:CH * w_], parts3[i][:, 0:CH * w_], ALU.subtract)\
                        .then_inc(msg_res, 1)

                def last_part(w, c, odd):
                    if k == 5:
                        return
                    i = (c + odd) % 2
                    n = CH * w_
                    dve.wait_ge(msg_mid, w * NC + (m * GB + c + 1))
                    V.tensor_tensor(parts3[i][:, 2 * n:3 * n], hid[i][:, 0:n], parts3[i][:, n:2 * n], ALU.subtract)\
                        .then_inc(msg_lo, 1)

                def second_part(w):
                    if later(w, 0, 1):
                        dve.wait_ge(y_stored, 16 * w + 16 * (2 + m * NB))
                    dve.wait_ge(agg_made, w * NC + (m * GB + NC))
                    dve.wait_ge(za_kept, w + (m * NB + 1))
                    V.tensor_tensor(ystage[:, 0:w_], y0[:, 0:w_], PS[:, 3584:3584 + w_], ALU.add).then_inc(zb_kept, 1)

                def body(w, odd, first=False):
                    for c in range(NC):
                        old = (w, c - 2, odd) if c >= 2 else None if first else (w - 1, NC + c - 2, 1 - odd)
                        if old:
                            gate(*old)
                        select_rows(w, c)
                        if old:
                            residual(*old)
                        select_sums(w, c)
                        if old:
                            last_part(*old)
                        if c == 4 and not first:
                            second_part(w - 1)
                blocks(dve, body)
                for c in range(NC - 2, NC):
                    gate(NB - 1, c, 0)
                    residual(NB - 1, c, 0)
                    last_part(NB - 1, c, 0)
                second_part(NB - 1)
                dve.wait_ge(agg_in[k], 16)

            def fast_or_general(k):
                with dve.If(fast):
                    (slots if k in SLOT_PASSES else product)(k)
                with dve.If(1 - fast):
                    edge_pass(k)
                    dve.wait_ge(agg_in[k], 16)

            TB3 = TB.rearrange("p (b f) -> p b f", b=NB)

            def sums(w):
                return AG[:, 0:NB * w].rearrange("p (b f) -> p b f", b=NB)

            dve.wait_ge(pool_const, 10)
            dve.wait_ge(x_in, 32)
            dve.wait_ge(weights_in, WEIGHTS)

            dve.wait_ge(lin_kept, 1)
            V.tensor_copy(TB3[:, :, 0:D], XR[:, :, :]).then_inc(tab_ready, 1)
            count_blocks()
            place_edges()
            make_counts()
            fast = dve.value_load(flag_i[0:1, 0:1], min_val=0, max_val=1)
            fast_or_general(0)
            step(V.tensor_copy(st[:, BDEG, :], sums(D + 1)[:, :, D:D + 1].rearrange("p b a -> p (b a)")))
            inverse(BINV, BDEG)
            dve.wait_ge(tab_stored[0], 16)
            step(V.memset(TB3[:, :, D:D + 1], 1.0))
            V.tensor_tensor(TB3[:, :, 0:D], sums(D + 1)[:, :, 0:D], per_node(BINV, D), ALU.mult).then_inc(tab_ready, 1)
            fast_or_general(1)
            step(V.tensor_copy(st[:, DDEG, :], sums(D + 1)[:, :, D:D + 1].rearrange("p b a -> p (b a)")))
            inverse(DINV, DDEG)
            V.tensor_tensor(NW[:, :, 0:D], sums(D + 1)[:, :, 0:D], per_node(DINV, D), ALU.mult).then_inc(lin_in, 1)
            keep("l0a", NW, relu=True)
            V.tensor_scalar(NW[:, :, 0:D], NW[:, :, 0:D], 1.0, None, ALU.mult).then_inc(tab_ready, 1)
            fast_or_general(2)
            V.tensor_tensor(NW[:, :, 0:D], sums(D), per_node(BINV, D), ALU.mult).then_inc(tab_ready, 1)
            fast_or_general(3)
            V.tensor_tensor(NW[:, :, 0:D], sums(D), per_node(DINV, D), ALU.mult).then_inc(lin_in, 1)
            keep("l0b", NW)
            step(V.tensor_tensor(XR[:, :, :], XR[:, :, :], NW[:, :, 0:D], ALU.add))
            layer_norm()

            V.memset(st[:, SUM, :], 0.0).then_inc(lin_in, 2)
            keep("l1p", NW)
            keep("l1q", NV)
            V.memset(st[:, SUM, :], 0.0).then_inc(tab_ready, 1)
            fast_or_general(4)
            V.memset(st[:, VAR, :], 0.0).then_inc(lin_in, 1)
            keep("l1s", NW)
            step(V.tensor_tensor(NV[:, :, 0:D], per_node(BDEG, D),
                                 be2b[:, :].rearrange("p (a f) -> p a f", a=1).to_broadcast((P, NB, D)), ALU.mult))
            V.tensor_tensor(NW[:, :, 0:D], NW[:, :, 0:D], NV[:, :, 0:D], ALU.add).then_inc(lin_in, 1)
            keep("l1h", NV, relu=True)
            V.memset(st[:, VAR, :], 0.0).then_inc(lin_in, 1)
            keep("l1o", NW)
            step(V.tensor_tensor(XR[:, :, :], XR[:, :, :], NW[:, :, 0:D], ALU.add))
            layer_norm()

            V.memset(st[:, SUM, :], 0.0).then_inc(lin_in, 2)
            keep("l2k", NW)
            keep("l2q", NV)
            step(V.tensor_copy(SK[:, :, :], NW[:, :, D:H]))
            V.memset(st[:, SUM, :], 0.0).then_inc(tab_ready, 1)
            fast_or_general(5)
            step(V.tensor_tensor(XR[:, :, :], XR[:, :, :], sums(D), ALU.add))
            step(V.tensor_tensor(XR[:, :, :], XR[:, :, :], SK[:, :, :], ALU.add))
            layer_norm()

            step(V.tensor_scalar(st[:, DDEG, :], st[:, DDEG, :], 1.0, None, ALU.add))
            step(V.tensor_scalar(st[:, DINV, :], st[:, DDEG, :], DEG_EPS, None, ALU.add))
            step(V.reciprocal(st[:, DINV, :], st[:, DINV, :]))
            V.tensor_tensor(st[:, SUM, :], st[:, DDEG, :], st[:, DINV, :], ALU.mult).then_inc(std_in, 1)
            root()
            step(V.reciprocal(st[:, SCL, :], st[:, TMP, :]))
            step(V.tensor_tensor(SK[:, :, :], XR[:, :, :], per_node(SCL, D), ALU.mult))
            V.tensor_copy(NW[:, :, 0:D], SK[:, :, :]).then_inc(tab_ready, 1)
            step(V.tensor_tensor(st[:, SCL, :], st[:, SCL, :], st[:, DINV, :], ALU.mult))
            fast_or_general(6)
            step(V.tensor_tensor(SK[:, :, :], SK[:, :, :], sums(D), ALU.add))
            step(V.tensor_tensor(SK[:, :, :], SK[:, :, :], per_node(SCL, D), ALU.mult))
            step(V.tensor_tensor(XR[:, :, :], XR[:, :, :], SK[:, :, :], ALU.add))
            layer_norm()
            V.memset(st[:, SUM, :], 0.0).then_inc(out_ready, 1)


_INS = ['x', 'src', 'dst', 'edge_attr_64', 'L0_gnn_W1', 'L0_gnn_b1', 'L0_gnn_W2', 'L0_gnn_b2',
        'L1_gnn_We1', 'L1_gnn_be1', 'L1_gnn_We2', 'L1_gnn_be2', 'L1_gnn_Wn1', 'L1_gnn_bn1', 'L1_gnn_Wn2', 'L1_gnn_bn2',
        'L2_gnn_W_key', 'L2_gnn_b_key', 'L2_gnn_W_query', 'L2_gnn_b_query', 'L2_gnn_W_value', 'L2_gnn_b_value',
        'L2_gnn_W_skip', 'L2_gnn_b_skip']
_OUTS = [((N, D), 'float32')]


def kernel(**inputs):
    import numpy as _np
    import concourse.bacc as _bacc
    from concourse import mybir as _mybir
    from concourse.bass_utils import run_bass_kernel_spmd as _run

    nc = _bacc.Bacc("TRN2", target_bir_lowering=False, num_devices=1)
    arrays, args = {}, []
    for name in _INS:
        a = _np.ascontiguousarray(inputs[name])
        arrays[f"in_{name}_dram"] = a
        args.append(nc.dram_tensor(f"in_{name}_dram", a.shape, _mybir.dt.from_np(a.dtype), kind="ExternalInput").ap())
    for i, (shape, dtype) in enumerate(_OUTS):
        dt = _mybir.dt.from_np(_np.dtype(dtype))
        args.append(nc.dram_tensor(f"out_{i}_dram", shape, dt, kind="ExternalOutput").ap())
    build(nc, *args)
    r = _run(nc, [arrays], core_ids=[0])
    return r.results[0]["out_0_dram"]
```
